# Optimizing a Trainium2 kernel written in Bass

```python
import numpy as np
import jax
import jax.numpy as jnp

def _softmax(x, axis=-1):
    return jax.nn.softmax(x, axis=axis)

def _gelu(x):
    return jax.nn.gelu(x, approximate=True)

def _silu(x):
    return jax.nn.silu(x)

def _sigmoid(x):
    return jax.nn.sigmoid(x)

def _layernorm(x, axis=-1, eps=1e-05):
    m = jnp.mean(x, axis=axis, keepdims=True)
    v = jnp.var(x, axis=axis, keepdims=True)
    return (x - m) / jnp.sqrt(v + eps)

def _scatter_add(tgt, idx, src, axis=0):
    return tgt.at[idx].add(src)

def _segment_sum(src, seg, n):
    return jax.ops.segment_sum(src, seg, n)
kernel_name = 'mk_xattn_ffn_d1_seqx_r4_37f202'

def setup_inputs(seed: int=0):
    np.random.seed(seed)
    _w = jnp.asarray

    def _rec_inputs():
        import jax
        import jax.numpy as jnp
        _rk = jax.random.key(seed)
        x = -0.0003929 + 0.9999 * jax.random.normal(jax.random.fold_in(_rk, 1), (8, 112, 256), jnp.float32)
        _lenS = 112 - jax.random.randint(jax.random.fold_in(_rk, 7), (8,), 0, max(1, 112 // 4) + 1, jnp.int32)
        _lenS2 = 375 - jax.random.randint(jax.random.fold_in(_rk, 8), (8,), 0, max(1, 375 // 4) + 1, jnp.int32)
        _ctx_1024P = jax.random.normal(jax.random.fold_in(_rk, 11), (8, 16, 256), jnp.float32)
        _ctx_1024c = jax.random.dirichlet(jax.random.fold_in(_rk, 511), 0.3 * jnp.ones((16,), jnp.float32), (8, 375))
        _ctx_1024t = jnp.einsum('bsk,bkd->bsd', _ctx_1024c, _ctx_1024P)
        _ctx_1024t = _ctx_1024t * jax.lax.rsqrt(jnp.mean(jnp.square(_ctx_1024t)) + 1e-12) * 0.953939
        ctx_1024 = 4.13588e-05 + 0.999923 * (_ctx_1024t + 0.3 * jax.random.normal(jax.random.fold_in(_rk, 611), (8, 375, 256), jnp.float32))
        return (x, ctx_1024)
    x, ctx_1024 = _rec_inputs()

    def _L0_xattn_setup():
        import jax, jax.numpy as jnp
        import numpy as np
        key = jax.random.key(seed)
        k1, k2 = jax.random.split(key)
        B, L, V, D = (8, 512, 256, 256)
        hidden_states = jax.random.normal(k1, (B, L, D), dtype=jnp.float32)
        visual_hidden_state = jax.random.normal(k2, (B, V, D), dtype=jnp.float32)
        return {'hidden_states': hidden_states, 'visual_hidden_state': visual_hidden_state}
    _L0_xattn_all = _L0_xattn_setup()
    _L0_xattn_in = {k: v for k, v in _L0_xattn_all.items() if k in ()}
    del _L0_xattn_all

    def _L0_ffn_setup():
        import jax, jax.numpy as jnp
        import numpy as np
        NUM_EXPERTS = 8
        N_EMBD = 256
        D_FF = 4 * N_EMBD
        B, S = (4, 512)
        key = jax.random.key(seed)
        ks = jax.random.split(key, 6)
        x = jax.random.normal(ks[0], (B, S, N_EMBD), dtype=jnp.float32)
        gate_w = jax.random.normal(ks[1], (N_EMBD, NUM_EXPERTS), dtype=jnp.float32) * 0.02
        w1 = jax.random.normal(ks[2], (NUM_EXPERTS, N_EMBD, D_FF), dtype=jnp.float32) * 0.02
        b1 = jnp.zeros((NUM_EXPERTS, D_FF), dtype=jnp.float32)
        w2 = jax.random.normal(ks[3], (NUM_EXPERTS, D_FF, N_EMBD), dtype=jnp.float32) * 0.02
        b2 = jnp.zeros((NUM_EXPERTS, N_EMBD), dtype=jnp.float32)
        return {'x': x, 'gate_w': gate_w, 'w1': w1, 'b1': b1, 'w2': w2, 'b2': b2}
    _L0_ffn_all = _L0_ffn_setup()
    _L0_ffn_in = {k: v for k, v in _L0_ffn_all.items() if k in ('gate_w', 'w1', 'b1', 'w2', 'b2')}
    del _L0_ffn_all
    return {'x': x, 'ctx_1024': ctx_1024, 'L0_ffn_gate_w': _L0_ffn_in['gate_w'], 'L0_ffn_w1': _L0_ffn_in['w1'], 'L0_ffn_b1': _L0_ffn_in['b1'], 'L0_ffn_w2': _L0_ffn_in['w2'], 'L0_ffn_b2': _L0_ffn_in['b2']}

def reference(x, ctx_1024, L0_ffn_gate_w, L0_ffn_w1, L0_ffn_b1, L0_ffn_w2, L0_ffn_b2):
    import jax
    import jax.numpy as jnp

    def _L0_xattn_ref(hidden_states, visual_hidden_state):
        import jax, jax.numpy as jnp
        import numpy as np
        scores = jnp.einsum('bld,bvd->blv', hidden_states, visual_hidden_state)
        probs = jax.nn.softmax(scores, axis=-1)
        return jnp.einsum('blv,bvd->bld', probs, visual_hidden_state)

    def _L0_ffn_ref(x, gate_w, w1, b1, w2, b2):
        import jax, jax.numpy as jnp
        import numpy as np
        NUM_EXPERTS = 8
        N_EMBD = 256
        D_FF = 4 * N_EMBD
        B, S = (4, 512)
        Bb, Ss, D = x.shape
        x_flat = x.reshape(-1, D)
        router_logits = x_flat @ gate_w
        router_probs = jax.nn.softmax(router_logits, axis=-1)
        expert_idx = jnp.argmax(router_probs, axis=-1)
        expert_w = jnp.take_along_axis(router_probs, expert_idx[:, None], axis=1)[:, 0]
        out = jnp.zeros_like(x_flat)
        for e in range(NUM_EXPERTS):
            h = jax.nn.gelu(x_flat @ w1[e] + b1[e], approximate=False)
            y = h @ w2[e] + b2[e]
            sel = expert_idx == e
            out = out + jnp.where(sel, expert_w, 0.0)[:, None] * y
        return out.reshape(Bb, Ss, D)
    x = x + _L0_xattn_ref(_layernorm(x, axis=-1), ctx_1024)
    x = x + _L0_ffn_ref(_layernorm(x, axis=-1), L0_ffn_gate_w, L0_ffn_w1, L0_ffn_b1, L0_ffn_w2, L0_ffn_b2)
    return x

_drawn_inputs = setup_inputs


def setup_inputs(seed=0):
    import zlib

    import numpy as np

    out = dict(_drawn_inputs(seed))
    spreads = {'L0_ffn_b1': (0.0, 0.8), 'L0_ffn_b2': (0.0, 0.678)}
    factors = {'L0_ffn_gate_w': 3.27, 'L0_ffn_w1': 4.435, 'L0_ffn_w2': 4.143}
    for name, (base, spread) in spreads.items():
        noise = np.random.default_rng([zlib.crc32(name.encode()), seed]).standard_normal(out[name].shape)
        drawn = base * np.exp(spread * noise) if base else spread * noise
        out[name] = jnp.asarray(drawn.astype(out[name].dtype))
    for name, factor in factors.items():
        out[name] = (out[name] * factor).astype(out[name].dtype)
    return out
```

```python
from contextlib import ExitStack

import concourse.bass as bass
from concourse import mybir

F32 = mybir.dt.float32
F16 = mybir.dt.float16
BF16 = mybir.dt.bfloat16
I32 = mybir.dt.int32
ALU = mybir.AluOpType
ACT = mybir.ActivationFunctionType
AX = mybir.AxisListType.X

P = 128
EPS = 1e-5
BIAS_PARTS = 3
SPLIT = 3
ROW = 260


def xattn_moe(nc, x, ctx_in, gate_w, w1, b1, w2, b2, out):
    B, L, D = x.shape
    V = ctx_in.shape[1]
    NE, _, F = w1.shape
    DC, FC = D // P, F // P
    VP = V // SPLIT
    T = B * L
    NT = (T + NE * (P - 1)) // P
    PASS = 1024
    COLS = 512
    assert D == DC * P and F == FC * P and VP * SPLIT == V and T < PASS and L <= P

    table = nc.dram_tensor("token_table", [T, ROW], F32).ap()
    b1_rows = nc.dram_tensor("b1_rows", [BIAS_PARTS, NE * F], BF16).ap()
    b2_rows = nc.dram_tensor("b2_rows", [BIAS_PARTS, NE * D], BF16).ap()
    BR = BIAS_PARTS * NE
    BW = NE * (F + D) // P
    out_rows = out.rearrange("b l d -> (b l) d")

    with ExitStack() as stack:
        def sb(name, shape, dt=F32):
            return stack.enter_context(nc.sbuf_tensor(name, shape, dt))

        def ps(name, shape, dt=F32):
            return stack.enter_context(nc.psum_tensor(name, shape, dt))

        def sem(name):
            return stack.enter_context(nc.semaphore(name))

        w1_sb = sb("w1_sb", [P, NE, DC, F])
        w2_sb = sb("w2_sb", [P, NE, FC, D])
        gate_sb = sb("gate_sb", [P, DC, NE])
        bias_sb = sb("bias_sb", [BR, F + D], BF16)
        row_expert = sb("row_expert", [BR, 1], I32)
        pick1 = sb("pick1", [BR, P], BF16)
        pick2 = sb("pick2", [BR, P], BF16)
        bias_f32 = sb("bias_f32", [P, BW])
        bias_rest = sb("bias_rest", [P, 2, BW])
        bias_split = sb("bias_split", [P, BIAS_PARTS, BW], BF16)
        ident = sb("ident", [P, P])
        before = sb("before", [L, P], F16)
        ones16 = sb("ones16", [L, P], F16)
        slot_iota = sb("slot_iota", [L, P])
        tile_iota = sb("tile_iota", [L, NT])
        expert_iota = sb("expert_iota", [L, NE])
        full_tiles = sb("full_tiles", [P, B])
        token_no = sb("token_no", [L, B])
        zeros = sb("zeros", [P, NE])
        x_sb = sb("x_sb", [L, B, D])
        ctx_room = sb("ctx_room", [P, B * SPLIT * D])
        ctx_sb = ctx_room[0:VP, :].rearrange("p (b t d) -> p b t d", t=SPLIT, d=D)
        ctx_stage = sb("ctx_stage", [VP, SPLIT, D])
        ctxT = sb("ctxT", [P, DC, SPLIT * VP])
        stat1 = sb("stat1", [L, 6])
        mv1 = sb("mv1", [L, 2])
        rstd1 = sb("rstd1", [L, 1])
        var1 = sb("var1", [L, 1])
        var2 = sb("var2", [L, 1])
        mv2 = sb("mv2", [L, 2])
        power = sb("power", [L, 1])
        xn = sb("xn", [L, D])
        xnT = sb("xnT", [P, DC, L])
        nmax = sb("nmax", [L, 1])
        probs = sb("probs", [L, SPLIT * VP])
        prob_sum = sb("prob_sum", [L, 1])
        prob_rec = sb("prob_rec", [L, 1])
        probsT = sb("probsT", [VP, SPLIT, L])
        tok = sb("tok", [L, B, ROW])
        stat2 = sb("stat2", [L, 6])
        x2n = sb("x2n", [L, D])
        x2T = sb("x2T", [P, DC, L])
        logits = sb("logits", [L, B, NE])
        lmax = sb("lmax", [L, B])
        nlmax = sb("nlmax", [L, 1])
        lexp = sb("lexp", [L, NE])
        lsum = sb("lsum", [L, 1])
        is_max = sb("is_max", [L, B, NE])
        keyed = sb("keyed", [L, B, NE])
        key = sb("key", [L, B])
        chosen = sb("chosen", [L, B, NE], F16)
        more = sb("more", [P, NE, B])
        ntiles = sb("ntiles", [P, NE])
        tile_end = sb("tile_end", [P, NE])
        tile_start = sb("tile_start", [P, NE])
        place = sb("place", [L, B, NE])
        mine = sb("mine", [L, B, NE])
        pos = sb("pos", [L, B])
        pos_i = sb("pos_i", [L, B], I32)
        slot_i = sb("slot_i", [L, B], I32)
        tile_i = sb("tile_i", [L, B], I32)
        slot_hot = sb("slot_hot", [L, B, P], F16)
        tile_hot = sb("tile_hot", [L, B, NT])
        tile_tok = sb("tile_tok", [L, B, NT], F16)
        past = sb("past", [BR, NT, NE])
        tile_expert = sb("tile_expert", [BR, NT])
        tile_expert_c = sb("tile_expert_c", [BR, NT])
        tile_expert_i = sb("tile_expert_i", [1, NT], I32)
        slot_token = sb("slot_token", [P, NT], I32)
        GB = 2
        rows = [sb(f"rows{i}", [P, ROW]) for i in range(GB)]
        act = ctx_room[:, 0:F]
        actT = ctx_room[:, F:2 * F].rearrange("p (c s) -> p c s", s=P)
        xs = ctx_room[:, 2 * F:2 * F + D]
        xsT = ctx_room[:, 2 * F + D:2 * F + 2 * D].rearrange("p (c s) -> p c s", s=P)
        kept_x1 = ctx_room[:, 2 * F + 2 * D:2 * F + (2 + NT) * D].rearrange("p (j d) -> p j d", d=D)
        kept_weight = sb("kept_weight", [P, NT])
        gather_from = [sb(f"gather_from{i}", [P, 1], I32) for i in range(GB)]
        scatter_to = [sb(f"scatter_to{i}", [P, 1], I32) for i in range(GB)]
        res = [sb(f"res{i}", [P, D]) for i in range(GB)]

        bank = [ps(f"bank{i}", [P, COLS]) for i in range(4)]
        pair = [ps(f"pair{i}", [P, 2 * COLS]) for i in range(2)]
        VN = SPLIT * VP
        ctxT_ps = pair[0]
        scores_ps = bank[0][0:L, 0:VN]
        probsT_ps = bank[1][0:VP, 0:SPLIT * L]
        values_ps = bank[2][0:L, 0:D]
        xnT_ps = bank[3][:, 0:DC * L]
        x2T_ps = pair[1][:, 0:DC * L]
        logit_ps = pair[1][0:L, COLS:COLS + NE]
        rank_ps = bank[0][:, 0:(B + 1) * NE]
        token_ps = bank[1][:, 0:NT]
        hid_ps = pair[0]
        actT_ps = pair[1]
        y_ps = bank[2][:, 0:D]
        xsT_ps = bank[3][:, 0:DC * P]

        x_head, x_tail, ctx_head, ctx_tail = (sem(n) for n in ("x_head", "x_tail", "ctx_head", "ctx_tail"))
        gate_loaded, bias_loaded = sem("gate_loaded"), sem("bias_loaded")
        bias_stored, bias_back, bias_cut = sem("bias_stored"), sem("bias_back"), sem("bias_cut")
        weights_loaded = sem("weights_loaded")
        consts_pool, consts_dve = sem("consts_pool"), sem("consts_dve")
        (staged, xn_stat, xn_mv, xn_rstd, xn_ready, transposed, xnT_ready, ctxT_lo, ctxT_hi, scored, max_ready,
         exp_ready, probs_turned, probsT_ready, valued, rec_ready, x1_ready, x2_stat, x2_mv, x2_rstd, x2_ready,
         x2_turned, x2T_ready, routed, logits_ready, lmax_ready, lexp_ready, weight_ready, row_stored) = (
            sem(n) for n in ("staged", "xn_stat", "xn_mv", "xn_rstd", "xn_ready", "transposed", "xnT_ready",
                             "ctxT_lo", "ctxT_hi", "scored", "max_ready", "exp_ready", "probs_turned",
                             "probsT_ready", "valued", "rec_ready", "x1_ready", "x2_stat", "x2_mv", "x2_rstd",
                             "x2_ready", "x2_turned", "x2T_ready", "routed", "logits_ready", "lmax_ready",
                             "lexp_ready", "weight_ready", "row_stored"))
        route, chosen_ready, ranked, hot_ready, listed, slots_ready, experts_ready = (
            sem(n) for n in ("route", "chosen_ready", "ranked", "hot_ready", "listed", "slots_ready",
                             "experts_ready"))
        (gathered0, gathered1, xs_ready, xs_turned, xsT_ready, hidden0, hidden1, gelu0, gelu1, act_turned0, act_turned1,
         actT_lo, actT_hi, projected, res_ready, scattered0, scattered1, rows_clear) = (
            sem(n) for n in ("gathered0", "gathered1", "xs_ready", "xs_turned", "xsT_ready", "hidden0", "hidden1", "gelu0",
                             "gelu1", "act_turned0", "act_turned1", "actT_lo", "actT_hi", "projected", "res_ready",
                             "scattered0", "scattered1", "rows_clear"))
        xn_var, x2_var, power_set = sem("xn_var"), sem("x2_var"), sem("power_set")
        indices_ready = sem("indices_ready")
        gathered, scattered = (gathered0, gathered1), (scattered0, scattered1)

        def after_wait(engine):
            engine.nop(nofuse=True)

        block = stack.enter_context(nc.Block())

        @block.sync
        def _(sp):
            HEAD = 2
            MAIN = VP - VP % 16
            by_part = ctx_in.rearrange("b (p t) d -> p b t d", t=SPLIT)
            x_v = x.rearrange("b l d -> l b d")
            sp.dma_start(x_sb[:, 0:HEAD, :], x_v[:, 0:HEAD, :]).then_inc(x_head, 16)
            for lo, hi, loaded in ((0, HEAD, ctx_head), (HEAD, B, ctx_tail)):
                sp.dma_start(ctx_sb[0:MAIN, lo:hi], by_part[0:MAIN, lo:hi]).then_inc(loaded, 16)
                sp.dma_start(ctx_sb[MAIN:VP, lo:hi], by_part[MAIN:VP, lo:hi]).then_inc(loaded, 16)
                if lo == 0:
                    sp.dma_start(x_sb[:, HEAD:B, :], x_v[:, HEAD:B, :]).then_inc(x_tail, 16)
            sp.dma_start(gate_sb[:], gate_w.rearrange("(c p) e -> p c e", p=P)).then_inc(gate_loaded, 16)
            with sp.Fori(0, NE) as e:
                sp.dma_start(w1_sb[:, e], w1[e].rearrange("(c p) f -> p c f", p=P)).then_inc(weights_loaded, 16)
                sp.dma_start(w2_sb[:, e], w2[e].rearrange("(c p) d -> p c d", p=P)).then_inc(weights_loaded, 16)

        @block.gpsimd
        def _(pool):
            pool.dma_start(bias_f32[:, 0:NE * F // P], b1.rearrange("e f -> (e f)").rearrange("(p n) -> p n", p=P)
                           ).then_inc(bias_loaded, 16)
            pool.dma_start(bias_f32[:, NE * F // P:BW], b2.rearrange("e f -> (e f)").rearrange("(p n) -> p n", p=P)
                           ).then_inc(bias_loaded, 16)
            pool.memset(ident[:], 0.0).then_inc(consts_pool, 1)
            pool.memset(before[:], 1.0).then_inc(consts_pool, 1)
            pool.wait_ge(consts_pool, 2)
            pool.affine_select(out=ident[:], in_=ident[:], compare_op=ALU.not_equal, fill=1.0, base=0,
                               pattern=[[-1, P]], channel_multiplier=1).then_inc(consts_pool, 1)

            def stage(b):
                pool.tensor_copy(ctx_stage[:], ctx_sb[:, b]).then_inc(staged, 1)

            def inverse_std1(b):
                pool.wait_ge(xn_var, b + 1)
                pool.tensor_tensor(rstd1[:], var1[:], power[:], ALU.pow).then_inc(xn_rstd, 1)

            def inverse_std2(b):
                pool.wait_ge(x2_var, b + 1)
                pool.tensor_copy(tok[:, b, D:D + 1], mv2[:, 0:1])
                pool.tensor_tensor(tok[:, b, D + 1:D + 2], var2[:], power[:], ALU.pow).then_inc(x2_rstd, 1)

            pool.wait_ge(power_set, 1)
            inverse_std1(0)
            pool.wait_ge(ctx_head, 32)
            stage(0)
            inverse_std1(1)
            pool.affine_select(out=before[:], in_=before[:], compare_op=ALU.is_gt, fill=0.0, base=0,
                               pattern=[[1, P]], channel_multiplier=-1).then_inc(consts_pool, 1)
            pool.memset(ones16[:], 1.0).then_inc(consts_pool, 1)
            pool.iota(row_expert[:], [[0, 1]], base=0, channel_multiplier=1).then_inc(consts_pool, 1)
            pool.iota(slot_iota[:], [[1, P]], base=0, channel_multiplier=0,
                      allow_small_or_imprecise_dtypes=True).then_inc(consts_pool, 1)
            pool.iota(tile_iota[:], [[1, NT]], base=0, channel_multiplier=0,
                      allow_small_or_imprecise_dtypes=True).then_inc(consts_pool, 1)
            pool.iota(expert_iota[:], [[1, NE]], base=-NE, channel_multiplier=0,
                      allow_small_or_imprecise_dtypes=True).then_inc(consts_pool, 1)
            pool.iota(full_tiles[:], [[P, B]], base=0, channel_multiplier=0,
                      allow_small_or_imprecise_dtypes=True).then_inc(consts_pool, 1)
            pool.iota(token_no[:], [[L, B]], base=-PASS, channel_multiplier=1,
                      allow_small_or_imprecise_dtypes=True).then_inc(consts_pool, 1)
            pool.memset(zeros[:], 0.0).then_inc(consts_pool, 1)
            for i in range(GB):
                pool.memset(rows[i][:], 0.0).then_inc(rows_clear, 1)
            pool.wait_ge(transposed, 1)
            stage(1)
            inverse_std1(2)
            pool.wait_ge(ctx_tail, 32)
            pool.wait_ge(transposed, 2)
            stage(2)
            inverse_std2(0)
            pool.wait_ge(bias_cut, 3)
            pool.dma_start(b1_rows.rearrange("t (p n) -> p t n", p=P), bias_split[:, :, 0:NE * F // P]
                           ).then_inc(bias_stored, 16)
            pool.dma_start(b2_rows.rearrange("t (p n) -> p t n", p=P), bias_split[:, :, NE * F // P:BW]
                           ).then_inc(bias_stored, 16)

            def store(b):
                pool.wait_ge(weight_ready, b + 1)
                pool.dma_start(table[bass.ts(b, L), :], tok[:, b, :]).then_inc(row_stored, 16)

            with pool.Fori(1, B - 2) as b:
                pool.wait_ge(transposed, b + 2)
                stage(b + 2)
                inverse_std1(b + 2)
                inverse_std2(b)
                store(b - 1)
            pool.wait_ge(bias_stored, 32)
            pool.dma_start(bias_sb[:, 0:F], b1_rows.rearrange("t (e f) -> (t e) f", f=F)).then_inc(bias_back, 16)
            pool.dma_start(bias_sb[:, F:F + D], b2_rows.rearrange("t (e f) -> (t e) f", f=D)).then_inc(bias_back, 16)
            inverse_std2(B - 2)
            store(B - 3)
            inverse_std2(B - 1)
            store(B - 2)
            store(B - 1)
            pool.wait_ge(row_stored, 16 * B)
            pool.wait_ge(slots_ready, 1)

            def indices(to, j):
                pool.tensor_copy(to[:], slot_token[:, bass.ds(j, 1)]).then_inc(indices_ready, 1)

            def gather(j, k, turn):
                if not (isinstance(turn, int) and turn == 0):
                    pool.wait_ge(gathered[k], 16 * turn)
                    pool.wait_ge(xs_ready, j - 1)
                indices(gather_from[k], j)
                pool.wait_ge(indices_ready, count_of(j))
                after_wait(pool)
                pool.indirect_dma_start(out=rows[k][:], out_offset=None, in_=table,
                                        in_offset=bass.IndirectOffsetOnAxis(ap=gather_from[k][:], axis=0),
                                        bounds_check=T - 1, oob_is_err=False).then_inc(gathered[k], 16)

            def scatter(j, k, turn, made):
                if not (isinstance(turn, int) and turn == 0):
                    pool.wait_ge(scattered[k], 16 * turn)
                indices(scatter_to[k], j)
                pool.wait_ge(indices_ready, made)
                pool.wait_ge(res_ready, j + 1)
                after_wait(pool)
                pool.indirect_dma_start(out=out_rows, in_=res[k][:], in_offset=None,
                                        out_offset=bass.IndirectOffsetOnAxis(ap=scatter_to[k][:], axis=0),
                                        bounds_check=T - 1, oob_is_err=False).then_inc(scattered[k], 16)

            AHEAD = 6
            assert AHEAD % GB == 0 and NT % GB == 0

            def count_of(j):
                return j + 1 if isinstance(j, int) and j < AHEAD else 2 * j - AHEAD + 2

            pool.wait_ge(rows_clear, GB)
            for j in range(AHEAD):
                gather(j, j % GB, j // GB)
            with pool.Fori(0, (NT - AHEAD) // GB) as i:
                for k in range(GB):
                    scatter(GB * i + k, k, i, AHEAD + 2 * (GB * i + k) + 1)
                    gather(GB * i + k + AHEAD, k, i + AHEAD // GB)
            for j in range(NT - AHEAD, NT):
                scatter(j, j % GB, j // GB, NT + j + 1)
            for k in range(GB):
                pool.wait_ge(scattered[k], 16 * (NT // GB))

        @block.tensor
        def _(pe):
            def turn(b):
                pe.wait_ge(staged, b + 1)
                for c in range(DC):
                    for t in range(SPLIT):
                        pe.transpose(ctxT_ps[:, c * COLS + t * VP:c * COLS + (t + 1) * VP],
                                     ctx_stage[:, t, bass.ts(c, P)], ident[0:VP, 0:VP])
                pe.wait_ge(xn_ready, b + 1)
                for c in range(DC):
                    last = pe.transpose(xnT_ps[:, bass.ts(c, L)], xn[:, bass.ts(c, P)], ident[0:L, 0:L])
                last.then_inc(transposed, 1)

            def score(b):
                pe.wait_ge(xnT_ready, b + 1)
                pe.wait_ge(ctxT_lo, b + 1)
                pe.wait_ge(ctxT_hi, b + 1)
                for c in range(DC):
                    last = pe.matmul(scores_ps, xnT[:, c, :], ctxT[:, c, :], start=(c == 0), stop=(c == DC - 1))
                last.then_inc(scored, 1)

            def turn_probs(b):
                pe.wait_ge(exp_ready, b + 1)
                for t in range(SPLIT):
                    last = pe.transpose(probsT_ps[:, bass.ts(t, L)], probs[:, bass.ts(t, VP)], ident[0:L, 0:L])
                last.then_inc(probs_turned, 1)

            def value(b):
                pe.wait_ge(probsT_ready, b + 1)
                for t in range(SPLIT):
                    last = pe.matmul(values_ps, probsT[:, t, :], ctx_sb[:, b, t, :],
                                     start=(t == 0), stop=(t == SPLIT - 1))
                last.then_inc(valued, 1)

            def turn_x2(b):
                pe.wait_ge(x2_ready, b + 1)
                for c in range(DC):
                    last = pe.transpose(x2T_ps[:, bass.ts(c, L)], x2n[:, bass.ts(c, P)], ident[0:L, 0:L])
                last.then_inc(x2_turned, 1)

            def router(b):
                pe.wait_ge(x2T_ready, b + 1)
                for c in range(DC):
                    last = pe.matmul(logit_ps, x2T[:, c, :], gate_sb[:, c, :], start=(c == 0), stop=(c == DC - 1))
                last.then_inc(routed, 1)

            pe.wait_ge(consts_pool, 3)
            turn(0)
            score(0)
            turn(1)
            turn_probs(0)
            score(1)
            value(0)
            pe.wait_ge(gate_loaded, 16)
            with pe.Fori(1, B - 1) as b:
                turn(b + 1)
                turn_probs(b)
                score(b + 1)
                turn_x2(b - 1)
                value(b)
                router(b - 1)
            turn_probs(B - 1)
            turn_x2(B - 2)
            value(B - 1)
            router(B - 2)
            turn_x2(B - 1)
            router(B - 1)

            pe.wait_ge(chosen_ready, 1)
            pe.wait_ge(consts_pool, 12)
            flat = chosen[:].rearrange("p b e -> p (b e)")
            pe.matmul(rank_ps[:, 0:B * NE], before[:], flat, start=True, stop=False, skip_group_check=True)
            for s in range(1, B + 1):
                last = pe.matmul(rank_ps[:, s * NE:(B + 1) * NE], ones16[:], flat[:, 0:(B + 1 - s) * NE],
                                 start=False, stop=(s == B), skip_group_check=True)
            last.then_inc(ranked, 1)

            pe.wait_ge(hot_ready, 1)
            for b in range(B):
                last = pe.matmul(token_ps, slot_hot[:, b, :], tile_tok[:, b, :], start=(b == 0), stop=(b == B - 1))
            last.then_inc(listed, 1)

            pe.wait_ge(bias_back, 32)
            pe.wait_ge(experts_ready, 2)
            pe.wait_ge(weights_loaded, 2 * 16 * NE)

            def turn_xs(j):
                pe.wait_ge(xs_ready, j + 1)
                for c in range(DC):
                    last = pe.transpose(xsT_ps[:, bass.ts(c, P)], xs[:, bass.ts(c, P)], ident[:])
                last.then_inc(xs_turned, 1)

            def layer1(j):
                e = pe.value_load(tile_expert_i[0:1, j:j + 1] if isinstance(j, int)
                                  else tile_expert_i[0:1, bass.ds(j, 1)], min_val=0, max_val=NE - 1)
                pe.wait_ge(xsT_ready, j + 1)
                for h, done in ((0, hidden0), (1, hidden1)):
                    cols = bass.ts(h, COLS)
                    pe.matmul(hid_ps[:, cols], pick1[:], bias_sb[:, cols], start=True, stop=False)
                    for c in range(DC):
                        last = pe.matmul(hid_ps[:, cols], xsT[:, c, :], w1_sb[:, e, c, cols], start=False,
                                         stop=(c == DC - 1))
                    last.then_inc(done, 1)

            def turn_act(j):
                half = FC // 2
                for c in range(FC):
                    if c == 0:
                        pe.wait_ge(gelu0, j + 1)
                    if c == half:
                        pe.wait_ge(gelu1, j + 1)
                    last = pe.transpose(actT_ps[:, bass.ts(c, P)], act[:, bass.ts(c, P)], ident[:])
                    if c == half - 1:
                        last.then_inc(act_turned0, 1)
                last.then_inc(act_turned1, 1)

            def layer2(j):
                e = pe.value_load(tile_expert_i[0:1, j:j + 1] if isinstance(j, int)
                                  else tile_expert_i[0:1, bass.ds(j, 1)], min_val=0, max_val=NE - 1)
                pe.wait_ge(actT_lo, j + 1)
                pe.matmul(y_ps, pick2[:], bias_sb[:, F:F + D], start=True, stop=False)
                for c in range(FC):
                    if c == FC // 2:
                        pe.wait_ge(actT_hi, j + 1)
                    last = pe.matmul(y_ps, actT[:, c, :], w2_sb[:, e, c, :], start=False, stop=(c == FC - 1))
                last.then_inc(projected, 1)

            turn_xs(0)
            layer1(0)
            turn_xs(1)
            turn_act(0)
            layer1(1)
            turn_xs(2)
            with pe.Fori(1, NT - 2) as j:
                layer2(j - 1)
                turn_act(j)
                layer1(j + 1)
                turn_xs(j + 2)
            layer2(NT - 3)
            turn_act(NT - 2)
            layer1(NT - 1)
            layer2(NT - 2)
            turn_act(NT - 1)
            layer2(NT - 1)

        @block.scalar
        def _(sc):
            def ctx_half(b):
                sc.wait_ge(transposed, b + 1)
                sc.activation(ctxT[:, 0, :], ctxT_ps[:, 0:VN], ACT.Copy).then_inc(ctxT_lo, 1)

            def exps(b):
                if not (isinstance(b, int) and b == 0):
                    sc.wait_ge(rec_ready, b)
                sc.wait_ge(max_ready, b + 1)
                sc.activation(probs[:], scores_ps, ACT.Exp, bias=nmax[:], scale=1.0,
                              accum_out=prob_sum[:]).then_inc(exp_ready, 1)

            def probs_back(b):
                sc.wait_ge(probs_turned, b + 1)
                sc.activation(probsT[:].rearrange("p t l -> p (t l)"), probsT_ps, ACT.Copy).then_inc(probsT_ready, 1)

            def logit_exps(b):
                if not (isinstance(b, int) and b == 0):
                    sc.wait_ge(weight_ready, b)
                sc.wait_ge(lmax_ready, b + 1)
                sc.activation(lexp[:], logits[:, b, :], ACT.Exp, bias=nlmax[:], scale=1.0,
                              accum_out=lsum[:]).then_inc(lexp_ready, 1)

            ctx_half(0)
            exps(0)
            ctx_half(1)
            probs_back(0)
            exps(1)
            with sc.Fori(1, B - 1) as b:
                ctx_half(b + 1)
                probs_back(b)
                exps(b + 1)
                logit_exps(b - 1)
            probs_back(B - 1)
            logit_exps(B - 2)
            logit_exps(B - 1)

            def gelus(j):
                sc.wait_ge(hidden0, j + 1)
                sc.activation(act[:, 0:COLS], hid_ps[:, 0:COLS], ACT.Gelu).then_inc(gelu0, 1)
                sc.wait_ge(hidden1, j + 1)
                sc.activation(act[:, COLS:F], hid_ps[:, COLS:F], ACT.Gelu).then_inc(gelu1, 1)

            def act_back(j):
                sc.wait_ge(act_turned1, j + 1)
                sc.activation(actT[:, FC // 2:FC, :].rearrange("p c s -> p (c s)"), actT_ps[:, COLS:F],
                              ACT.Copy).then_inc(actT_hi, 1)

            gelus(0)
            with sc.Fori(0, NT - 1) as j:
                act_back(j)
                gelus(j + 1)
            act_back(NT - 1)

        @block.vector
        def _(dve):
            dve.memset(power[:], -0.5).then_inc(power_set, 1)
            dve.wait_ge(x_head, 16)

            def normalise(b):
                dve.bn_stats(stat1[:], x_sb[:, b, :]).then_inc(xn_stat, 1)
                dve.wait_ge(xn_stat, b + 1)
                after_wait(dve)
                dve.bn_aggr(mv1[:], stat1[:]).then_inc(xn_mv, 1)
                dve.wait_ge(xn_mv, b + 1)
                dve.tensor_scalar(var1[:], mv1[:, 1:2], EPS, None, ALU.add).then_inc(xn_var, 1)
                dve.wait_ge(xn_rstd, b + 1)
                if not (isinstance(b, int) and b == 0):
                    dve.wait_ge(transposed, b)
                dve.tensor_scalar(xn[:], x_sb[:, b, :], mv1[:, 0:1], rstd1[:, 0:1], ALU.subtract,
                                  ALU.mult).then_inc(xn_ready, 1)

            def inputs_back(b):
                dve.wait_ge(transposed, b + 1)
                dve.tensor_copy(xnT[:].rearrange("p c l -> p (c l)"), xnT_ps).then_inc(xnT_ready, 1)
                dve.tensor_copy(ctxT[:, 1, :], ctxT_ps[:, COLS:COLS + VN]).then_inc(ctxT_hi, 1)

            def score_max(b):
                dve.wait_ge(scored, b + 1)
                dve.tensor_reduce(nmax[:], scores_ps, AX, ALU.max, negate=True).then_inc(max_ready, 1)

            def reciprocal_sum(b):
                dve.wait_ge(exp_ready, b + 1)
                dve.reciprocal(prob_rec[:], prob_sum[:]).then_inc(rec_ready, 1)

            def residual(b):
                dve.wait_ge(rec_ready, b + 1)
                dve.wait_ge(valued, b + 1)
                dve.scalar_tensor_tensor(out=tok[:, b, 0:D], in0=values_ps, scalar=prob_rec[:, 0:1],
                                         in1=x_sb[:, b, :], op0=ALU.mult, op1=ALU.add).then_inc(x1_ready, 1)
                dve.wait_ge(x1_ready, b + 1)
                after_wait(dve)
                dve.bn_stats(stat2[:], tok[:, b, 0:D]).then_inc(x2_stat, 1)
                dve.wait_ge(x2_stat, b + 1)
                after_wait(dve)
                dve.bn_aggr(mv2[:], stat2[:]).then_inc(x2_mv, 1)
                dve.wait_ge(x2_mv, b + 1)
                dve.tensor_scalar(var2[:], mv2[:, 1:2], EPS, None, ALU.add).then_inc(x2_var, 1)
                dve.wait_ge(x2_rstd, b + 1)
                dve.tensor_scalar(x2n[:], tok[:, b, 0:D], mv2[:, 0:1], tok[:, b, D + 1:D + 2], ALU.subtract,
                                  ALU.mult).then_inc(x2_ready, 1)

            def x2_back(b):
                dve.wait_ge(x2_turned, b + 1)
                dve.tensor_copy(x2T[:].rearrange("p c l -> p (c l)"), x2T_ps).then_inc(x2T_ready, 1)

            def logits_back(b):
                dve.wait_ge(routed, b + 1)
                dve.tensor_copy(logits[:, b, :], logit_ps).then_inc(logits_ready, 1)
                dve.tensor_reduce(lmax[:, b:b + 1] if isinstance(b, int) else lmax[:, bass.ds(b, 1)], logit_ps, AX,
                                  ALU.max).then_inc(logits_ready, 1)
                dve.tensor_reduce(nlmax[:], logit_ps, AX, ALU.max, negate=True).then_inc(lmax_ready, 1)

            def weight(b):
                dve.wait_ge(lexp_ready, b + 1)
                dve.reciprocal(tok[:, b, D + 2:D + 3], lsum[:]).then_inc(weight_ready, 1)

            dve.memset(tok[:, :, D + 3:ROW], 0.0).then_inc(consts_dve, 1)
            normalise(0)
            inputs_back(0)
            normalise(1)
            score_max(0)
            dve.wait_ge(bias_loaded, 32)
            dve.tensor_copy(bias_split[:, 0, :], bias_f32[:]).then_inc(bias_cut, 1)
            inputs_back(1)
            dve.wait_ge(x_tail, 16)
            normalise(2)
            reciprocal_sum(0)
            score_max(1)
            dve.wait_ge(bias_cut, 1)
            dve.tensor_tensor(bias_rest[:, 0, :], bias_f32[:], bias_split[:, 0, :], ALU.subtract).then_inc(consts_dve, 1)
            residual(0)
            dve.wait_ge(consts_dve, 2)
            dve.tensor_copy(bias_split[:, 1, :], bias_rest[:, 0, :]).then_inc(bias_cut, 1)
            dve.wait_ge(bias_cut, 2)
            dve.tensor_tensor(bias_rest[:, 1, :], bias_rest[:, 0, :], bias_split[:, 1, :],
                              ALU.subtract).then_inc(consts_dve, 1)
            dve.wait_ge(consts_dve, 3)
            dve.tensor_copy(bias_split[:, 2, :], bias_rest[:, 1, :]).then_inc(bias_cut, 1)
            dve.wait_ge(consts_pool, 12)
            dve.tensor_scalar(row_expert[:], row_expert[:], NE - 1, None, ALU.bitwise_and).then_inc(bias_cut, 1)
            with dve.Fori(1, B - 2) as b:
                inputs_back(b + 1)
                normalise(b + 2)
                reciprocal_sum(b)
                score_max(b + 1)
                x2_back(b - 1)
                residual(b)
                logits_back(b - 1)
                weight(b - 1)
            inputs_back(B - 1)
            reciprocal_sum(B - 2)
            score_max(B - 1)
            x2_back(B - 3)
            residual(B - 2)
            logits_back(B - 3)
            weight(B - 3)
            x2_back(B - 2)
            reciprocal_sum(B - 1)
            residual(B - 1)
            logits_back(B - 2)
            weight(B - 2)
            x2_back(B - 1)
            logits_back(B - 1)

            steps = 0

            def result(ins):
                nonlocal steps
                steps += 1
                ins.then_inc(route, 1)
                return steps

            def over(ap, n):
                return ap.unsqueeze(2).to_broadcast([ap.shape[0], ap.shape[1], n])

            def under(ap, n):
                return ap.unsqueeze(1).to_broadcast([ap.shape[0], n, ap.shape[1]])

            dve.wait_ge(consts_pool, 12)
            dve.wait_ge(logits_ready, 2 * B)
            s = result(dve.tensor_tensor(is_max[:], logits[:], over(lmax[:], NE), ALU.is_ge))
            weight(B - 1)
            dve.wait_ge(route, s)
            s = result(dve.tensor_tensor(keyed[:], is_max[:], under(expert_iota[:], B), ALU.mult))
            dve.wait_ge(route, s)
            s = result(dve.tensor_reduce(key[:], keyed[:], AX, ALU.min))
            dve.wait_ge(route, s)
            dve.tensor_tensor(chosen[:], under(expert_iota[:], B), over(key[:], NE), ALU.is_equal).then_inc(chosen_ready, 1)
            dve.wait_ge(ranked, 1)
            s = result(dve.tensor_tensor(more[:], over(rank_ps[:, B * NE:(B + 1) * NE], B), under(full_tiles[:], NE),
                                         ALU.is_gt))
            dve.wait_ge(route, s)
            s = result(dve.tensor_reduce(ntiles[:], more[:], AX, ALU.add))
            dve.wait_ge(route, s)
            s = result(dve.tensor_tensor_scan(tile_end[:], ntiles[:], zeros[:], 0.0, ALU.add, ALU.add))
            dve.wait_ge(route, s)
            s = result(dve.tensor_tensor(tile_start[:], tile_end[:], ntiles[:], ALU.subtract))
            dve.wait_ge(route, s)
            s = result(dve.scalar_tensor_tensor(out=place[:], in0=under(tile_start[0:L, :], B), scalar=float(P),
                                                in1=rank_ps[0:L, 0:B * NE].rearrange("p (b e) -> p b e", e=NE),
                                                op0=ALU.mult, op1=ALU.add))
            dve.wait_ge(route, s)
            dve.wait_ge(chosen_ready, 1)
            s = result(dve.tensor_tensor(mine[:], place[:], chosen[:], ALU.mult))
            dve.wait_ge(route, s)
            s = result(dve.tensor_reduce(pos[:], mine[:], AX, ALU.add))
            dve.wait_ge(route, s)
            s = result(dve.tensor_copy(pos_i[:], pos[:]))
            dve.wait_ge(route, s)
            result(dve.tensor_scalar(tile_i[:], pos_i[:], 7, None, ALU.logical_shift_right))
            s = result(dve.tensor_scalar(slot_i[:], pos_i[:], P - 1, None, ALU.bitwise_and))
            dve.wait_ge(route, s)
            s = result(dve.tensor_tensor(tile_hot[:], under(tile_iota[:], B), over(tile_i[:], NT), ALU.is_equal))
            result(dve.tensor_tensor(slot_hot[:], under(slot_iota[:], B), over(slot_i[:], P), ALU.is_equal))
            dve.wait_ge(route, s + 1)
            dve.tensor_tensor(tile_tok[:], tile_hot[:], over(token_no[:], NT), ALU.mult).then_inc(hot_ready, 1)
            s = result(dve.tensor_tensor(past[:], over(tile_iota[0:BR, :], NE), under(tile_end[0:BR, :], NT), ALU.is_ge))
            dve.wait_ge(route, s)
            s = result(dve.tensor_reduce(tile_expert[:], past[:], AX, ALU.add))
            dve.wait_ge(route, s)
            dve.tensor_scalar(tile_expert_c[:], tile_expert[:], float(NE - 1), None, ALU.min).then_inc(experts_ready, 1)
            dve.tensor_scalar(tile_expert_i[:], tile_expert[0:1, :], float(NE - 1), None, ALU.min).then_inc(experts_ready, 1)
            dve.wait_ge(bias_cut, 4)
            dve.wait_ge(listed, 1)
            dve.tensor_scalar(slot_token[:], token_ps, float(PASS), None, ALU.add).then_inc(slots_ready, 1)

            def pick(rows_of, j):
                dve.tensor_scalar(rows_of[:], row_expert[:].to_broadcast([BR, P]), tile_expert_c[:, bass.ds(j, 1)], None,
                                  ALU.is_equal)

            dve.wait_ge(experts_ready, 2)

            def tile_in(j, k, turn):
                dve.wait_ge(gathered[k], 16 * turn + 16)
                dve.tensor_copy(kept_x1[:, bass.ds(j, 1), :].rearrange("p a d -> p (a d)"), rows[k][:, 0:D])
                dve.tensor_copy(kept_weight[:, bass.ds(j, 1)], rows[k][:, D + 2:D + 3])
                if not (isinstance(j, int) and j == 0):
                    dve.wait_ge(xs_turned, j)
                dve.tensor_scalar(xs, rows[k][:, 0:D], rows[k][:, D:D + 1], rows[k][:, D + 1:D + 2],
                                  ALU.subtract, ALU.mult).then_inc(xs_ready, 1)

            def xs_back(j):
                dve.wait_ge(xs_turned, j + 1)
                if not (isinstance(j, int) and j == 0):
                    dve.wait_ge(hidden1, j)
                pick(pick1, j)
                dve.tensor_copy(xsT.rearrange("p c s -> p (c s)"), xsT_ps).then_inc(xsT_ready, 1)

            def act_back(j):
                dve.wait_ge(act_turned0, j + 1)
                pick(pick2, j)
                dve.tensor_copy(actT[:, 0:FC // 2, :].rearrange("p c s -> p (c s)"), actT_ps[:, 0:COLS]
                                ).then_inc(actT_lo, 1)

            def result_out(j, k, turn):
                dve.wait_ge(projected, j + 1)
                if not (isinstance(turn, int) and turn == 0):
                    dve.wait_ge(scattered[k], 16 * turn)
                dve.scalar_tensor_tensor(out=res[k][:], in0=y_ps, scalar=kept_weight[:, bass.ds(j, 1)],
                                         in1=kept_x1[:, bass.ds(j, 1), :].rearrange("p a d -> p (a d)"),
                                         op0=ALU.mult, op1=ALU.add).then_inc(res_ready, 1)

            tile_in(0, 0, 0)
            xs_back(0)
            tile_in(1, 1, 0)
            xs_back(1)
            tile_in(2, 0, 1)
            act_back(0)
            xs_back(2)
            tile_in(3, 1, 1)
            with dve.Fori(0, (NT - 4) // GB) as i:
                for k in range(GB):
                    result_out(GB * i + k, k, i)
                    act_back(GB * i + k + 1)
                    xs_back(GB * i + k + 3)
                    tile_in(GB * i + k + 4, k, i + 2)
            result_out(NT - 4, 0, NT // GB - 2)
            act_back(NT - 3)
            xs_back(NT - 1)
            result_out(NT - 3, 1, NT // GB - 2)
            act_back(NT - 2)
            result_out(NT - 2, 0, NT // GB - 1)
            act_back(NT - 1)
            result_out(NT - 1, 1, NT // GB - 1)


_INS = ['x', 'ctx_1024', 'L0_ffn_gate_w', 'L0_ffn_w1', 'L0_ffn_b1', 'L0_ffn_w2', 'L0_ffn_b2']


def kernel(**inputs):
    import numpy as _np
    import concourse.bacc as _bacc
    from concourse.bass_utils import run_bass_kernel_spmd as _run

    nc = _bacc.Bacc("TRN2", target_bir_lowering=False, num_devices=1)
    arrays, args = {}, []
    for name in _INS:
        a = _np.ascontiguousarray(inputs[name])
        arrays[f"in_{name}_dram"] = a
        args.append(nc.dram_tensor(f"in_{name}_dram", a.shape, mybir.dt.from_np(a.dtype), kind="ExternalInput").ap())
    shape = arrays["in_x_dram"].shape
    args.append(nc.dram_tensor("out_0_dram", shape, F32, kind="ExternalOutput").ap())
    xattn_moe(nc, *args)
    r = _run(nc, [arrays], core_ids=[0])
    return r.results[0]["out_0_dram"]
```

```python
from contextlib import ExitStack

import concourse.bass as bass
from concourse import mybir

F32 = mybir.dt.float32
F16 = mybir.dt.float16
BF16 = mybir.dt.bfloat16
I32 = mybir.dt.int32
ALU = mybir.AluOpType
ACT = mybir.ActivationFunctionType
AX = mybir.AxisListType.X

P = 128
EPS = 1e-5
BIAS_PARTS = 3
SPLIT = 3
ROW = 260


def xattn_moe(nc, x, ctx_in, gate_w, w1, b1, w2, b2, out):
    B, L, D = x.shape
    V = ctx_in.shape[1]
    NE, _, F = w1.shape
    DC, FC = D // P, F // P
    VP = V // SPLIT
    T = B * L
    NT = (T + NE * (P - 1)) // P
    LEAST = -(-T // P)
    HEAD = 2
    CONSTS = 12
    PASS = 1024
    COLS = 512
    assert D == DC * P and F == FC * P and VP * SPLIT == V and T < PASS and L <= P

    table = nc.dram_tensor("token_table", [T, ROW], F32).ap()
    b1_rows = nc.dram_tensor("b1_rows", [BIAS_PARTS, NE * F], BF16).ap()
    b2_rows = nc.dram_tensor("b2_rows", [BIAS_PARTS, NE * D], BF16).ap()
    BR = BIAS_PARTS * NE
    BW = NE * (F + D) // P
    out_rows = out.rearrange("b l d -> (b l) d")

    with ExitStack() as stack:
        def sb(name, shape, dt=F32):
            return stack.enter_context(nc.sbuf_tensor(name, shape, dt))

        def ps(name, shape, dt=F32):
            return stack.enter_context(nc.psum_tensor(name, shape, dt))

        def sem(name):
            return stack.enter_context(nc.semaphore(name))

        w1_sb = sb("w1_sb", [P, NE, DC, F])
        w2_sb = sb("w2_sb", [P, NE, FC, D])
        gate_sb = sb("gate_sb", [P, DC, NE])
        bias_sb = sb("bias_sb", [BR, F + D], BF16)
        row_expert = sb("row_expert", [BR, 1], I32)
        pick1 = sb("pick1", [BR, P], BF16)
        pick2 = sb("pick2", [BR, P], BF16)
        bias_f32 = sb("bias_f32", [P, BW])
        bias_rest = sb("bias_rest", [P, 2, BW])
        bias_split = sb("bias_split", [P, BIAS_PARTS, BW], BF16)
        ident = sb("ident", [P, P])
        before = sb("before", [L, P], F16)
        ones16 = sb("ones16", [L, P], F16)
        slot_iota = sb("slot_iota", [L, P])
        tile_iota = sb("tile_iota", [L, NT])
        expert_iota = sb("expert_iota", [L, NE])
        full_tiles = sb("full_tiles", [P, B])
        token_no = sb("token_no", [L, B])
        zeros = sb("zeros", [P, NE])
        x_sb = sb("x_sb", [L, B, D])
        ctx_room = sb("ctx_room", [P, B * SPLIT * D])
        ctx_sb = ctx_room[0:VP, :].rearrange("p (b t d) -> p b t d", t=SPLIT, d=D)
        ctx_stage = sb("ctx_stage", [VP, SPLIT, D])
        ctxT = sb("ctxT", [P, DC, SPLIT * VP])
        stat1 = sb("stat1", [L, B, 6])
        mv1 = sb("mv1", [L, B, 2])
        var1 = sb("var1", [L, B])
        rstd1 = sb("rstd1", [L, B])
        var2 = sb("var2", [L, 1])
        mv2 = sb("mv2", [L, 2])
        power = sb("power", [L, B])
        xn = sb("xn", [L, D])
        xnT = sb("xnT", [P, DC, L])
        nmax = sb("nmax", [L, 1])
        probs = sb("probs", [L, SPLIT * VP])
        prob_sum = sb("prob_sum", [L, 1])
        prob_rec = sb("prob_rec", [L, 1])
        probsT = sb("probsT", [VP, SPLIT, L])
        tok = sb("tok", [L, B, ROW])
        stat2 = sb("stat2", [L, 6])
        x2n = sb("x2n", [L, D])
        x2T = sb("x2T", [P, DC, L])
        logits = sb("logits", [L, B, NE])
        lmax = sb("lmax", [L, B])
        nlmax = sb("nlmax", [L, 1])
        lexp = sb("lexp", [L, NE])
        lsum = sb("lsum", [L, 1])
        is_max = sb("is_max", [L, B, NE])
        keyed = sb("keyed", [L, B, NE])
        key = sb("key", [L, B])
        chosen = sb("chosen", [L, B, NE], F16)
        more = sb("more", [P, NE, B])
        ntiles = sb("ntiles", [P, NE])
        tile_end = sb("tile_end", [P, NE])
        tile_start = sb("tile_start", [P, NE])
        place = sb("place", [L, B, NE])
        mine = sb("mine", [L, B, NE])
        pos = sb("pos", [L, B])
        pos_i = sb("pos_i", [L, B], I32)
        slot_i = sb("slot_i", [L, B], I32)
        tile_i = sb("tile_i", [L, B], I32)
        slot_hot = sb("slot_hot", [L, B, P], F16)
        tile_hot = sb("tile_hot", [L, B, NT])
        tile_tok = sb("tile_tok", [L, B, NT], F16)
        past = sb("past", [BR, NT, NE])
        tile_expert = sb("tile_expert", [BR, NT])
        tile_expert_c = sb("tile_expert_c", [BR, NT])
        tile_expert_i = sb("tile_expert_i", [1, NT], I32)
        tiles_left = sb("tiles_left", [1, NE], I32)
        slot_token = sb("slot_token", [P, NT], I32)
        act = ctx_room[:, 0:F]
        actT = ctx_room[:, F:2 * F].rearrange("p (c s) -> p c s", s=P)
        xs = ctx_room[:, 2 * F:2 * F + D]
        xsT = ctx_room[:, 2 * F + D:2 * F + 2 * D].rearrange("p (c s) -> p c s", s=P)
        rows = sb("rows", [P, ROW])
        res = sb("res", [P, D])
        kept_x1 = ctx_room[:, 2 * F + 2 * D:2 * F + (2 + NT) * D].rearrange("p (j d) -> p j d", d=D)
        kept_weight = sb("kept_weight", [P, NT])
        gather_from = sb("gather_from", [P, 1], I32)
        scatter_to = sb("scatter_to", [P, 1], I32)

        bank = [ps(f"bank{i}", [P, COLS]) for i in range(4)]
        pair = [ps(f"pair{i}", [P, 2 * COLS]) for i in range(2)]
        VN = SPLIT * VP
        ctxT_ps = pair[0]
        scores_ps = bank[0][0:L, 0:VN]
        probsT_ps = bank[1][0:VP, 0:SPLIT * L]
        values_ps = bank[2][0:L, 0:D]
        xnT_ps = bank[3][:, 0:DC * L]
        x2T_ps = pair[1][:, 0:DC * L]
        logit_ps = pair[1][0:L, COLS:COLS + NE]
        rank_ps = bank[0][:, 0:(B + 1) * NE]
        token_ps = bank[1][:, 0:NT]
        hid_ps = pair[0]
        actT_ps = pair[1]
        y_ps = bank[2][:, 0:D]
        xsT_ps = bank[3][:, 0:DC * P]

        x_head, x_tail, ctx_head, ctx_tail = (sem(n) for n in ("x_head", "x_tail", "ctx_head", "ctx_tail"))
        gate_loaded, bias_loaded = sem("gate_loaded"), sem("bias_loaded")
        bias_stored, bias_back, bias_cut = sem("bias_stored"), sem("bias_back"), sem("bias_cut")
        w1_loaded, w2_loaded = sem("w1_loaded"), sem("w2_loaded")
        experts_loaded = sem("experts_loaded")
        consts_pool, consts_dve = sem("consts_pool"), sem("consts_dve")
        (staged, xn_stat, xn_mv, xn_rstd, xn_ready, ctx_turned, xn_turned, xnT_ready, ctxT_ready, scored, max_ready,
         exp_ready, probs_turned, probsT_ready, valued, rec_ready, x1_ready, x2_stat, x2_mv, x2_rstd, x2_ready,
         x2_turned, x2T_ready, routed, logits_ready, lmax_ready, lexp_ready, weight_ready, row_stored) = (
            sem(n) for n in ("staged", "xn_stat", "xn_mv", "xn_rstd", "xn_ready", "ctx_turned", "xn_turned", "xnT_ready",
                             "ctxT_ready", "scored", "max_ready", "exp_ready", "probs_turned",
                             "probsT_ready", "valued", "rec_ready", "x1_ready", "x2_stat", "x2_mv", "x2_rstd",
                             "x2_ready", "x2_turned", "x2T_ready", "routed", "logits_ready", "lmax_ready",
                             "lexp_ready", "weight_ready", "row_stored"))
        route, chosen_ready, ranked, hot_ready, listed, slots_ready, experts_ready = (
            sem(n) for n in ("route", "chosen_ready", "ranked", "hot_ready", "listed", "slots_ready",
                             "experts_ready"))
        (gathered, xs_ready, xs_turned, xsT_ready, hidden0, hidden1, gelu0, gelu1, act_turned0, act_turned1,
         actT_lo, actT_hi, projected, res_ready, scattered, rows_clear) = (
            sem(n) for n in ("gathered", "xs_ready", "xs_turned", "xsT_ready", "hidden0", "hidden1", "gelu0",
                             "gelu1", "act_turned0", "act_turned1", "actT_lo", "actT_hi", "projected", "res_ready",
                             "scattered", "rows_clear"))
        xn_var, x2_var, power_set = sem("xn_var"), sem("x2_var"), sem("power_set")
        mean_kept = sem("mean_kept")
        indices_ready = sem("indices_ready")

        def after_wait(engine):
            engine.nop(nofuse=True)

        block = stack.enter_context(nc.Block())

        def at_least(n, least):
            return not isinstance(n, int) or n >= least

        def below(n, end):
            return not isinstance(n, int) or n < end

        def tiles_but(engine, n):
            return engine.value_load(tiles_left[0:1, NE - n:NE - n + 1], min_val=LEAST - n, max_val=NT - n)

        @block.sync
        def _(sp):
            MAIN = VP - VP % 16
            by_part = ctx_in.rearrange("b (p t) d -> p b t d", t=SPLIT)
            x_v = x.rearrange("b l d -> l b d")
            sp.dma_start(x_sb[:, 0:HEAD, :], x_v[:, 0:HEAD, :]).then_inc(x_head, 16)
            for lo, hi, loaded in ((0, HEAD, ctx_head), (HEAD, B, ctx_tail)):
                sp.dma_start(ctx_sb[0:MAIN, lo:hi], by_part[0:MAIN, lo:hi]).then_inc(loaded, 16)
                sp.dma_start(ctx_sb[MAIN:VP, lo:hi], by_part[MAIN:VP, lo:hi]).then_inc(loaded, 16)
                if lo == 0:
                    sp.dma_start(x_sb[:, HEAD:B, :], x_v[:, HEAD:B, :]).then_inc(x_tail, 16)
            sp.dma_start(gate_sb[:], gate_w.rearrange("(c p) e -> p c e", p=P)).then_inc(gate_loaded, 16)

            def load_expert(e):
                if at_least(e, 1):
                    sp.wait_ge(w1_loaded, 16 * e)
                sp.dma_start(w1_sb[:, e], w1[e].rearrange("(c p) f -> p c f", p=P)).then_inc(w1_loaded, 16)
                if at_least(e, 1):
                    sp.wait_ge(w2_loaded, 16 * e)
                    sp.sem_inc(experts_loaded, 1)
                sp.dma_start(w2_sb[:, e], w2[e].rearrange("(c p) d -> p c d", p=P)).then_inc(w2_loaded, 16)

            load_expert(0)
            with sp.Fori(1, NE) as e:
                load_expert(e)
            sp.wait_ge(w1_loaded, 16 * NE)
            sp.wait_ge(w2_loaded, 16 * NE)
            sp.sem_inc(experts_loaded, 1)

        @block.gpsimd
        def _(pool):
            pool.memset(ident[:], 0.0).then_inc(consts_pool, 1)
            pool.wait_ge(consts_pool, 1)
            pool.affine_select(out=ident[:], in_=ident[:], compare_op=ALU.not_equal, fill=1.0, base=0,
                               pattern=[[-1, P]], channel_multiplier=1).then_inc(consts_pool, 1)

            def inverse_std2(b):
                pool.wait_ge(x2_var, b + 1)
                pool.tensor_tensor(tok[:, b, D + 1:D + 2], var2[:], power[:, 0:1], ALU.pow).then_inc(x2_rstd, 1)
                pool.tensor_copy(tok[:, b, D:D + 1], mv2[:, 0:1]).then_inc(mean_kept, 1)

            def store(b):
                pool.wait_ge(mean_kept, b + 1)
                pool.wait_ge(weight_ready, b + 1)
                pool.dma_start(table[bass.ts(b, L), :], tok[:, b, :]).then_inc(row_stored, 16)

            pool.wait_ge(power_set, 1)
            pool.wait_ge(xn_var, 1)
            pool.tensor_tensor(rstd1[:, 0:HEAD], var1[:, 0:HEAD], power[:, 0:HEAD], ALU.pow).then_inc(xn_rstd, 1)
            pool.memset(before[:], 1.0).then_inc(consts_pool, 1)
            pool.wait_ge(consts_pool, 3)
            pool.affine_select(out=before[:], in_=before[:], compare_op=ALU.is_gt, fill=0.0, base=0,
                               pattern=[[1, P]], channel_multiplier=-1).then_inc(consts_pool, 1)
            pool.wait_ge(xn_var, 2)
            pool.tensor_tensor(rstd1[:, HEAD:B], var1[:, HEAD:B], power[:, HEAD:B], ALU.pow).then_inc(xn_rstd, 1)
            pool.memset(ones16[:], 1.0).then_inc(consts_pool, 1)
            pool.iota(row_expert[:], [[0, 1]], base=0, channel_multiplier=1).then_inc(consts_pool, 1)
            pool.iota(slot_iota[:], [[1, P]], base=0, channel_multiplier=0,
                      allow_small_or_imprecise_dtypes=True).then_inc(consts_pool, 1)
            pool.iota(tile_iota[:], [[1, NT]], base=0, channel_multiplier=0,
                      allow_small_or_imprecise_dtypes=True).then_inc(consts_pool, 1)
            pool.iota(expert_iota[:], [[1, NE]], base=-NE, channel_multiplier=0,
                      allow_small_or_imprecise_dtypes=True).then_inc(consts_pool, 1)
            pool.iota(full_tiles[:], [[P, B]], base=0, channel_multiplier=0,
                      allow_small_or_imprecise_dtypes=True).then_inc(consts_pool, 1)
            pool.iota(token_no[:], [[L, B]], base=-PASS, channel_multiplier=1,
                      allow_small_or_imprecise_dtypes=True).then_inc(consts_pool, 1)
            inverse_std2(0)
            pool.memset(zeros[:], 0.0).then_inc(consts_pool, 1)
            pool.memset(rows[:], 0.0).then_inc(rows_clear, 1)
            inverse_std2(1)
            inverse_std2(2)
            inverse_std2(3)
            pool.wait_ge(bias_cut, 3)
            pool.dma_start(b1_rows.rearrange("t (p n) -> p t n", p=P), bias_split[:, :, 0:NE * F // P]
                           ).then_inc(bias_stored, 16)
            store(0)
            inverse_std2(4)
            pool.dma_start(b2_rows.rearrange("t (p n) -> p t n", p=P), bias_split[:, :, NE * F // P:BW]
                           ).then_inc(bias_stored, 16)
            store(1)
            with pool.Fori(5, B) as b:
                inverse_std2(b)
                store(b - 3)
            pool.wait_ge(bias_stored, 32)
            pool.dma_start(bias_sb[:, 0:F], b1_rows.rearrange("t (e f) -> (t e) f", f=F)).then_inc(bias_back, 16)
            pool.dma_start(bias_sb[:, F:F + D], b2_rows.rearrange("t (e f) -> (t e) f", f=D)).then_inc(bias_back, 16)
            store(B - 3)
            store(B - 2)
            store(B - 1)
            pool.wait_ge(row_stored, 16 * B)
            pool.wait_ge(slots_ready, 1)

            def indices(to, j, made):
                pool.tensor_copy(to[:], slot_token[:, bass.ds(j, 1)]).then_inc(indices_ready, 1)
                pool.wait_ge(indices_ready, made)
                after_wait(pool)

            def gather(j, made):
                if at_least(j, 1):
                    pool.wait_ge(gathered, 16 * j)
                    pool.wait_ge(xs_ready, j)
                indices(gather_from, j, made)
                pool.indirect_dma_start(out=rows[:], out_offset=None, in_=table,
                                        in_offset=bass.IndirectOffsetOnAxis(ap=gather_from[:], axis=0),
                                        bounds_check=T - 1, oob_is_err=False).then_inc(gathered, 16)

            def scatter(j, made):
                if at_least(j, 1):
                    pool.wait_ge(scattered, 16 * j)
                pool.wait_ge(res_ready, j + 1)
                indices(scatter_to, j, made)
                pool.indirect_dma_start(out=out_rows, in_=res[:], in_offset=None,
                                        out_offset=bass.IndirectOffsetOnAxis(ap=scatter_to[:], axis=0),
                                        bounds_check=T - 1, oob_is_err=False).then_inc(scattered, 16)

            AHEAD = 5
            pool.wait_ge(rows_clear, 1)
            for j in range(AHEAD):
                gather(j, j + 1)
            most = tiles_but(pool, AHEAD)
            with pool.Fori(0, NT - AHEAD) as j:
                with pool.If(j < most):
                    scatter(j, 2 * j + AHEAD + 1)
                    gather(j + AHEAD, 2 * j + AHEAD + 2)
            for n in range(AHEAD):
                scatter(most + n, 2 * most + AHEAD + n + 1)
            pool.wait_ge(scattered, 16 * most + 16 * AHEAD)

        @block.tensor
        def _(pe):
            def turn(b):
                pe.wait_ge(staged, b + 1)
                if at_least(b, 1):
                    pe.wait_ge(ctxT_ready, 2 * b)
                for c in range(DC):
                    for t in range(SPLIT):
                        last = pe.transpose(ctxT_ps[:, c * COLS + t * VP:c * COLS + (t + 1) * VP],
                                            ctx_stage[:, t, bass.ts(c, P)], ident[0:VP, 0:VP])
                last.then_inc(ctx_turned, 1)
                pe.wait_ge(xn_ready, b + 1)
                for c in range(DC):
                    last = pe.transpose(xnT_ps[:, bass.ts(c, L)], xn[:, bass.ts(c, P)], ident[0:L, 0:L])
                last.then_inc(xn_turned, 1)

            def score(b):
                pe.wait_ge(ctxT_ready, 2 * b + 2)
                pe.wait_ge(xnT_ready, b + 1)
                for c in range(DC):
                    last = pe.matmul(scores_ps, xnT[:, c, :], ctxT[:, c, :], start=(c == 0), stop=(c == DC - 1))
                last.then_inc(scored, 1)

            def turn_probs(b):
                pe.wait_ge(exp_ready, b + 1)
                for t in range(SPLIT):
                    last = pe.transpose(probsT_ps[:, bass.ts(t, L)], probs[:, bass.ts(t, VP)], ident[0:L, 0:L])
                last.then_inc(probs_turned, 1)

            def value(b):
                pe.wait_ge(probsT_ready, b + 1)
                if at_least(b, 1):
                    pe.wait_ge(x1_ready, b)
                for t in range(SPLIT):
                    last = pe.matmul(values_ps, probsT[:, t, :], ctx_sb[:, b, t, :],
                                     start=(t == 0), stop=(t == SPLIT - 1))
                last.then_inc(valued, 1)

            def turn_x2(b):
                pe.wait_ge(x2_ready, b + 1)
                for c in range(DC):
                    last = pe.transpose(x2T_ps[:, bass.ts(c, L)], x2n[:, bass.ts(c, P)], ident[0:L, 0:L])
                last.then_inc(x2_turned, 1)

            def router(b):
                pe.wait_ge(x2T_ready, b + 1)
                if at_least(b, 1):
                    pe.wait_ge(lmax_ready, b)
                for c in range(DC):
                    last = pe.matmul(logit_ps, x2T[:, c, :], gate_sb[:, c, :], start=(c == 0), stop=(c == DC - 1))
                last.then_inc(routed, 1)

            def step(b):
                turn_probs(b)
                if below(b + 1, B):
                    score(b + 1)
                if below(b + 2, B):
                    turn(b + 2)
                value(b)
                if at_least(b - 2, 0):
                    router(b - 2)
                if at_least(b - 1, 0):
                    turn_x2(b - 1)

            pe.wait_ge(consts_pool, 2)
            turn(0)
            score(0)
            turn(1)
            step(0)
            step(1)
            pe.wait_ge(gate_loaded, 16)
            with pe.Fori(2, B - 2) as b:
                step(b)
            step(B - 2)
            step(B - 1)
            router(B - 2)
            turn_x2(B - 1)
            router(B - 1)

            pe.wait_ge(chosen_ready, 1)
            pe.wait_ge(consts_pool, CONSTS)
            flat = chosen[:].rearrange("p b e -> p (b e)")
            pe.matmul(rank_ps[:, 0:B * NE], before[:], flat, start=True, stop=False, skip_group_check=True)
            for s in range(1, B + 1):
                last = pe.matmul(rank_ps[:, s * NE:(B + 1) * NE], ones16[:], flat[:, 0:(B + 1 - s) * NE],
                                 start=False, stop=(s == B), skip_group_check=True)
            last.then_inc(ranked, 1)

            pe.wait_ge(hot_ready, 1)
            for b in range(B):
                last = pe.matmul(token_ps, slot_hot[:, b, :], tile_tok[:, b, :], start=(b == 0), stop=(b == B - 1))
            last.then_inc(listed, 1)

            def expert_of(j):
                return pe.value_load(tile_expert_i[0:1, bass.ds(j, 1)], min_val=0, max_val=NE - 1)

            def turn_xs(j):
                pe.wait_ge(xs_ready, j + 1)
                for c in range(DC):
                    last = pe.transpose(xsT_ps[:, bass.ts(c, P)], xs[:, bass.ts(c, P)], ident[:])
                last.then_inc(xs_turned, 1)

            def layer1(j):
                e = expert_of(j)
                pe.wait_ge(experts_loaded, e + 1)
                pe.wait_ge(xsT_ready, j + 1)
                for h, done in ((0, hidden0), (1, hidden1)):
                    cols = bass.ts(h, COLS)
                    pe.matmul(hid_ps[:, cols], pick1[:], bias_sb[:, cols], start=True, stop=False)
                    for c in range(DC):
                        last = pe.matmul(hid_ps[:, cols], xsT[:, c, :], w1_sb[:, e, c, cols], start=False,
                                         stop=(c == DC - 1))
                    last.then_inc(done, 1)

            def turn_act(j):
                half = FC // 2
                for c in range(FC):
                    if c == 0:
                        pe.wait_ge(gelu0, j + 1)
                    if c == half:
                        pe.wait_ge(gelu1, j + 1)
                    last = pe.transpose(actT_ps[:, bass.ts(c, P)], act[:, bass.ts(c, P)], ident[:])
                    if c == half - 1:
                        last.then_inc(act_turned0, 1)
                last.then_inc(act_turned1, 1)

            def layer2(j):
                e = expert_of(j)
                pe.wait_ge(actT_lo, j + 1)
                pe.matmul(y_ps, pick2[:], bias_sb[:, F:F + D], start=True, stop=False)
                for c in range(FC):
                    if c == FC // 2:
                        pe.wait_ge(actT_hi, j + 1)
                    last = pe.matmul(y_ps, actT[:, c, :], w2_sb[:, e, c, :], start=False, stop=(c == FC - 1))
                last.then_inc(projected, 1)

            pe.wait_ge(bias_back, 32)
            pe.wait_ge(experts_ready, 3)
            third = tiles_but(pe, 3)
            second, final = third + 1, third + 2
            turn_xs(0)
            layer1(0)
            turn_xs(1)
            turn_act(0)
            layer1(1)
            turn_xs(2)
            with pe.Fori(1, NT - 2) as j:
                with pe.If(j < second):
                    layer2(j - 1)
                    turn_act(j)
                    layer1(j + 1)
                    turn_xs(j + 2)
            layer2(third)
            turn_act(second)
            layer1(final)
            layer2(second)
            turn_act(final)
            layer2(final)

        @block.scalar
        def _(sc):
            for lo, hi, bias in ((0, NE * F // P, b1), (NE * F // P, BW, b2)):
                sc.dma_start(bias_f32[:, lo:hi], bias.rearrange("e f -> (e f)").rearrange("(p n) -> p n", p=P)
                             ).then_inc(bias_loaded, 16)

            def ctx_back(b):
                sc.wait_ge(ctx_turned, b + 1)
                if at_least(b, 1):
                    sc.wait_ge(scored, b)
                for c in range(DC):
                    sc.activation(ctxT[:, c, :], ctxT_ps[:, c * COLS:c * COLS + VN], ACT.Copy).then_inc(ctxT_ready, 1)

            def xn_back(b):
                sc.wait_ge(xn_turned, b + 1)
                sc.activation(xnT[:].rearrange("p c l -> p (c l)"), xnT_ps, ACT.Copy).then_inc(xnT_ready, 1)

            def exps(b):
                if at_least(b, 1):
                    sc.wait_ge(rec_ready, b)
                sc.wait_ge(max_ready, b + 1)
                sc.activation(probs[:], scores_ps, ACT.Exp, bias=nmax[:], scale=1.0,
                              accum_out=prob_sum[:]).then_inc(exp_ready, 1)

            def probs_back(b):
                sc.wait_ge(probs_turned, b + 1)
                sc.activation(probsT[:].rearrange("p t l -> p (t l)"), probsT_ps, ACT.Copy).then_inc(probsT_ready, 1)

            def x2_back(b):
                sc.wait_ge(x2_turned, b + 1)
                sc.activation(x2T[:].rearrange("p c l -> p (c l)"), x2T_ps, ACT.Copy).then_inc(x2T_ready, 1)

            def logit_exps(b):
                if at_least(b, 1):
                    sc.wait_ge(weight_ready, b)
                sc.wait_ge(lmax_ready, b + 1)
                sc.activation(lexp[:], logits[:, b, :], ACT.Exp, bias=nlmax[:], scale=1.0,
                              accum_out=lsum[:]).then_inc(lexp_ready, 1)

            def step(b):
                probs_back(b)
                if below(b + 2, B):
                    ctx_back(b + 2)
                if below(b + 1, B):
                    exps(b + 1)
                if below(b + 2, B):
                    xn_back(b + 2)
                if at_least(b - 2, 0):
                    logit_exps(b - 2)
                if at_least(b - 1, 0):
                    x2_back(b - 1)

            ctx_back(0)
            xn_back(0)
            exps(0)
            ctx_back(1)
            xn_back(1)
            step(0)
            step(1)
            with sc.Fori(2, B - 2) as b:
                step(b)
            step(B - 2)
            step(B - 1)
            logit_exps(B - 2)
            x2_back(B - 1)
            logit_exps(B - 1)

            def gelus(j):
                sc.wait_ge(hidden0, j + 1)
                sc.activation(act[:, 0:COLS], hid_ps[:, 0:COLS], ACT.Gelu).then_inc(gelu0, 1)
                sc.wait_ge(hidden1, j + 1)
                sc.activation(act[:, COLS:F], hid_ps[:, COLS:F], ACT.Gelu).then_inc(gelu1, 1)

            def act_back(j):
                sc.wait_ge(act_turned1, j + 1)
                sc.activation(actT[:, FC // 2:FC, :].rearrange("p c s -> p (c s)"), actT_ps[:, COLS:F],
                              ACT.Copy).then_inc(actT_hi, 1)

            sc.wait_ge(experts_ready, 3)
            final = tiles_but(sc, 1)
            gelus(0)
            with sc.Fori(0, NT - 1) as j:
                with sc.If(j < final):
                    act_back(j)
                    gelus(j + 1)
            act_back(final)

        @block.vector
        def _(dve):
            def statistics(lo, hi):
                for b in range(lo, hi):
                    dve.bn_stats(stat1[:, b, :], x_sb[:, b, :]).then_inc(xn_stat, 1)
                for b in range(lo, hi):
                    dve.wait_ge(xn_stat, b + 1)
                    dve.bn_aggr(mv1[:, b, :], stat1[:, b, :]).then_inc(xn_mv, 1)
                dve.wait_ge(xn_mv, hi)
                dve.tensor_scalar(var1[:, lo:hi], mv1[:, lo:hi, 1], EPS, None, ALU.add).then_inc(xn_var, 1)

            def normalise(b):
                if at_least(b, 1):
                    dve.wait_ge(xn_turned, b)
                dve.tensor_scalar(xn[:], x_sb[:, b, :], mv1[:, b, 0:1], rstd1[:, bass.ds(b, 1)], ALU.subtract,
                                  ALU.mult).then_inc(xn_ready, 1)

            def stage(b):
                if at_least(b, 1):
                    dve.wait_ge(ctx_turned, b)
                dve.tensor_copy(ctx_stage[:], ctx_sb[:, b]).then_inc(staged, 1)

            def score_max(b):
                dve.wait_ge(scored, b + 1)
                dve.tensor_reduce(nmax[:], scores_ps, AX, ALU.max, negate=True).then_inc(max_ready, 1)

            def reciprocal_sum(b):
                dve.wait_ge(exp_ready, b + 1)
                dve.reciprocal(prob_rec[:], prob_sum[:]).then_inc(rec_ready, 1)

            def residual(b, between):
                dve.wait_ge(rec_ready, b + 1)
                dve.wait_ge(valued, b + 1)
                dve.scalar_tensor_tensor(out=tok[:, b, 0:D], in0=values_ps, scalar=prob_rec[:, 0:1],
                                         in1=x_sb[:, b, :], op0=ALU.mult, op1=ALU.add).then_inc(x1_ready, 1)
                dve.wait_ge(x1_ready, b + 1)
                after_wait(dve)
                dve.bn_stats(stat2[:], tok[:, b, 0:D]).then_inc(x2_stat, 1)
                dve.wait_ge(x2_stat, b + 1)
                if at_least(b, 1):
                    dve.wait_ge(mean_kept, b)
                after_wait(dve)
                dve.bn_aggr(mv2[:], stat2[:]).then_inc(x2_mv, 1)
                dve.wait_ge(x2_mv, b + 1)
                dve.tensor_scalar(var2[:], mv2[:, 1:2], EPS, None, ALU.add).then_inc(x2_var, 1)
                between()
                dve.wait_ge(x2_rstd, b + 1)
                if at_least(b, 1):
                    dve.wait_ge(x2_turned, b)
                dve.tensor_scalar(x2n[:], tok[:, b, 0:D], mv2[:, 0:1], tok[:, b, D + 1:D + 2], ALU.subtract,
                                  ALU.mult).then_inc(x2_ready, 1)

            def logits_back(b):
                dve.wait_ge(routed, b + 1)
                if at_least(b, 1):
                    dve.wait_ge(lexp_ready, b)
                dve.tensor_reduce(nlmax[:], logit_ps, AX, ALU.max, negate=True).then_inc(logits_ready, 1)
                dve.tensor_reduce(lmax[:, bass.ds(b, 1)], logit_ps, AX, ALU.max).then_inc(logits_ready, 1)
                dve.tensor_copy(logits[:, b, :], logit_ps).then_inc(lmax_ready, 1)

            def weight(b):
                dve.wait_ge(lexp_ready, b + 1)
                dve.reciprocal(tok[:, b, D + 2:D + 3], lsum[:]).then_inc(weight_ready, 1)

            def step(b):
                if below(b + 1, B):
                    score_max(b + 1)
                if below(b + 3, B):
                    stage(b + 3)
                    normalise(b + 3)

                def between():
                    if at_least(b - 2, 0):
                        logits_back(b - 2)
                    if at_least(b - 3, 0):
                        weight(b - 3)
                residual(b, between)
                if below(b + 1, B):
                    reciprocal_sum(b + 1)

            dve.memset(power[:], -0.5).then_inc(power_set, 1)
            dve.memset(tok[:, :, D + 3:ROW], 0.0).then_inc(consts_dve, 1)
            dve.wait_ge(x_head, 16)
            statistics(0, HEAD)
            dve.wait_ge(ctx_head, 32)
            stage(0)
            dve.wait_ge(xn_rstd, 1)
            normalise(0)
            stage(1)
            normalise(1)
            dve.wait_ge(x_tail, 16)
            statistics(HEAD, B)
            score_max(0)
            dve.wait_ge(bias_loaded, 32)
            dve.tensor_copy(bias_split[:, 0, :], bias_f32[:]).then_inc(bias_cut, 1)
            dve.wait_ge(ctx_tail, 32)
            stage(2)
            dve.wait_ge(xn_rstd, 2)
            normalise(2)
            reciprocal_sum(0)
            step(0)
            dve.wait_ge(bias_cut, 1)
            dve.tensor_tensor(bias_rest[:, 0, :], bias_f32[:], bias_split[:, 0, :], ALU.subtract).then_inc(consts_dve, 1)
            step(1)
            dve.wait_ge(consts_dve, 2)
            dve.tensor_copy(bias_split[:, 1, :], bias_rest[:, 0, :]).then_inc(bias_cut, 1)
            dve.wait_ge(bias_cut, 2)
            dve.tensor_tensor(bias_rest[:, 1, :], bias_rest[:, 0, :], bias_split[:, 1, :],
                              ALU.subtract).then_inc(consts_dve, 1)
            step(2)
            dve.wait_ge(consts_dve, 3)
            dve.tensor_copy(bias_split[:, 2, :], bias_rest[:, 1, :]).then_inc(bias_cut, 1)
            dve.wait_ge(consts_pool, CONSTS)
            dve.tensor_scalar(row_expert[:], row_expert[:], NE - 1, None, ALU.bitwise_and).then_inc(bias_cut, 1)
            with dve.Fori(3, B - 3) as b:
                step(b)
            for b in range(B - 3, B):
                step(b)
            weight(B - 3)
            logits_back(B - 2)
            weight(B - 2)
            logits_back(B - 1)

            steps = 0

            def result(ins):
                nonlocal steps
                steps += 1
                ins.then_inc(route, 1)
                return steps

            def over(ap, n):
                return ap.unsqueeze(2).to_broadcast([ap.shape[0], ap.shape[1], n])

            def under(ap, n):
                return ap.unsqueeze(1).to_broadcast([ap.shape[0], n, ap.shape[1]])

            dve.wait_ge(logits_ready, 2 * B)
            dve.wait_ge(lmax_ready, B)
            s = result(dve.tensor_tensor(is_max[:], logits[:], over(lmax[:], NE), ALU.is_ge))
            dve.wait_ge(route, s)
            s = result(dve.tensor_tensor(keyed[:], is_max[:], under(expert_iota[:], B), ALU.mult))
            dve.wait_ge(route, s)
            s = result(dve.tensor_reduce(key[:], keyed[:], AX, ALU.min))
            dve.wait_ge(route, s)
            dve.tensor_tensor(chosen[:], under(expert_iota[:], B), over(key[:], NE), ALU.is_equal).then_inc(chosen_ready, 1)
            weight(B - 1)
            dve.wait_ge(ranked, 1)
            s = result(dve.tensor_tensor(more[:], over(rank_ps[:, B * NE:(B + 1) * NE], B), under(full_tiles[:], NE),
                                         ALU.is_gt))
            dve.wait_ge(route, s)
            s = result(dve.tensor_reduce(ntiles[:], more[:], AX, ALU.add))
            dve.wait_ge(route, s)
            s = result(dve.tensor_tensor_scan(tile_end[:], ntiles[:], zeros[:], 0.0, ALU.add, ALU.add))
            dve.wait_ge(route, s)
            s = result(dve.tensor_tensor(tile_start[:], tile_end[:], ntiles[:], ALU.subtract))
            dve.wait_ge(route, s)
            s = result(dve.scalar_tensor_tensor(out=place[:], in0=under(tile_start[0:L, :], B), scalar=float(P),
                                                in1=rank_ps[0:L, 0:B * NE].rearrange("p (b e) -> p b e", e=NE),
                                                op0=ALU.mult, op1=ALU.add))
            dve.wait_ge(route, s)
            dve.wait_ge(chosen_ready, 1)
            s = result(dve.tensor_tensor(mine[:], place[:], chosen[:], ALU.mult))
            dve.wait_ge(route, s)
            s = result(dve.tensor_reduce(pos[:], mine[:], AX, ALU.add))
            dve.wait_ge(route, s)
            s = result(dve.tensor_copy(pos_i[:], pos[:]))
            dve.wait_ge(route, s)
            result(dve.tensor_scalar(tile_i[:], pos_i[:], 7, None, ALU.logical_shift_right))
            s = result(dve.tensor_scalar(slot_i[:], pos_i[:], P - 1, None, ALU.bitwise_and))
            dve.wait_ge(route, s)
            s = result(dve.tensor_tensor(tile_hot[:], under(tile_iota[:], B), over(tile_i[:], NT), ALU.is_equal))
            result(dve.tensor_tensor(slot_hot[:], under(slot_iota[:], B), over(slot_i[:], P), ALU.is_equal))
            dve.wait_ge(route, s + 1)
            dve.tensor_tensor(tile_tok[:], tile_hot[:], over(token_no[:], NT), ALU.mult).then_inc(hot_ready, 1)
            s = result(dve.tensor_tensor(past[:], over(tile_iota[0:BR, :], NE), under(tile_end[0:BR, :], NT), ALU.is_ge))
            dve.wait_ge(listed, 1)
            dve.tensor_scalar(slot_token[:], token_ps, float(PASS), None, ALU.add).then_inc(slots_ready, 1)
            dve.wait_ge(route, s)
            s = result(dve.tensor_reduce(tile_expert[:], past[:], AX, ALU.add))
            dve.tensor_scalar(tiles_left[:], expert_iota[0:1, :], tile_end[0:1, NE - 1:NE], None, ALU.add).then_inc(experts_ready, 1)
            dve.wait_ge(route, s)
            dve.tensor_scalar(tile_expert_c[:], tile_expert[:], float(NE - 1), None, ALU.min).then_inc(experts_ready, 1)
            dve.tensor_scalar(tile_expert_i[:], tile_expert[0:1, :], float(NE - 1), None, ALU.min).then_inc(experts_ready, 1)
            dve.wait_ge(bias_cut, 4)
            dve.wait_ge(experts_ready, 3)
            fourth = tiles_but(dve, 4)
            third, second, final = fourth + 1, fourth + 2, fourth + 3

            def pick(rows_of, j):
                dve.tensor_scalar(rows_of[:], row_expert[:].to_broadcast([BR, P]), tile_expert_c[:, bass.ds(j, 1)], None,
                                  ALU.is_equal)

            def tile_in(j):
                dve.wait_ge(gathered, 16 * j + 16)
                dve.tensor_copy(kept_x1[:, bass.ds(j, 1), :].rearrange("p a d -> p (a d)"), rows[:, 0:D])
                dve.tensor_copy(kept_weight[:, bass.ds(j, 1)], rows[:, D + 2:D + 3])
                if at_least(j, 1):
                    dve.wait_ge(xs_turned, j)
                dve.tensor_scalar(xs, rows[:, 0:D], rows[:, D:D + 1], rows[:, D + 1:D + 2],
                                  ALU.subtract, ALU.mult).then_inc(xs_ready, 1)

            def xs_back(j):
                dve.wait_ge(xs_turned, j + 1)
                if at_least(j, 1):
                    dve.wait_ge(hidden1, j)
                pick(pick1, j)
                dve.tensor_copy(xsT.rearrange("p c s -> p (c s)"), xsT_ps).then_inc(xsT_ready, 1)

            def act_back(j):
                dve.wait_ge(act_turned0, j + 1)
                pick(pick2, j)
                dve.tensor_copy(actT[:, 0:FC // 2, :].rearrange("p c s -> p (c s)"), actT_ps[:, 0:COLS]
                                ).then_inc(actT_lo, 1)

            def result_out(j):
                dve.wait_ge(projected, j + 1)
                if at_least(j, 1):
                    dve.wait_ge(scattered, 16 * j)
                dve.scalar_tensor_tensor(out=res[:], in0=y_ps, scalar=kept_weight[:, bass.ds(j, 1)],
                                         in1=kept_x1[:, bass.ds(j, 1), :].rearrange("p a d -> p (a d)"),
                                         op0=ALU.mult, op1=ALU.add).then_inc(res_ready, 1)

            tile_in(0)
            xs_back(0)
            tile_in(1)
            xs_back(1)
            tile_in(2)
            act_back(0)
            xs_back(2)
            tile_in(3)
            with dve.Fori(1, NT - 3) as j:
                with dve.If(j < third):
                    result_out(j - 1)
                    act_back(j)
                    xs_back(j + 2)
                    tile_in(j + 3)
            result_out(fourth)
            act_back(third)
            xs_back(final)
            result_out(third)
            act_back(second)
            result_out(second)
            act_back(final)
            result_out(final)


_INS = ['x', 'ctx_1024', 'L0_ffn_gate_w', 'L0_ffn_w1', 'L0_ffn_b1', 'L0_ffn_w2', 'L0_ffn_b2']


def kernel(**inputs):
    import numpy as _np
    import concourse.bacc as _bacc
    from concourse.bass_utils import run_bass_kernel_spmd as _run

    nc = _bacc.Bacc("TRN2", target_bir_lowering=False, num_devices=1)
    arrays, args = {}, []
    for name in _INS:
        a = _np.ascontiguousarray(inputs[name])
        arrays[f"in_{name}_dram"] = a
        args.append(nc.dram_tensor(f"in_{name}_dram", a.shape, mybir.dt.from_np(a.dtype), kind="ExternalInput").ap())
    shape = arrays["in_x_dram"].shape
    args.append(nc.dram_tensor("out_0_dram", shape, F32, kind="ExternalOutput").ap())
    xattn_moe(nc, *args)
    r = _run(nc, [arrays], core_ids=[0])
    return r.results[0]["out_0_dram"]
```

```python
from contextlib import ExitStack, nullcontext

import concourse.bass as bass
from concourse import mybir

F32 = mybir.dt.float32
F16 = mybir.dt.float16
I32 = mybir.dt.int32
ALU = mybir.AluOpType
ACT = mybir.ActivationFunctionType
AX = mybir.AxisListType.X

P = 128
TILE = 144
EPS = 1e-5
SPLIT = 3


def xattn_moe(nc, x, ctx_in, gate_w, w1, b1, w2, b2, out):
    B, L, D = x.shape
    V = ctx_in.shape[1]
    NE, _, F = w1.shape
    DC, FC = D // P, F // P
    VP = V // SPLIT
    T = B * L
    NT = (T + NE * (TILE - 1)) // TILE
    LEAST = -(-T // TILE)
    HEAD = 2
    DIRECT = 4
    CONSTS = 13
    ROW = D + 2
    PAIRS = (NT + 1) // 2
    NX = 2 * PAIRS + 3
    HALF = TILE // 2
    NH = 2 * NX
    SHIFT = 18
    PER_HALF = -(-(1 << SHIFT) // HALF)
    assert all(n * PER_HALF >> SHIFT == n // HALF for n in range(NT * TILE)) and NT * TILE * PER_HALF < 1 << 24
    PEELED = (LEAST - 1) // 2 * 2
    SCALE = 4096.0
    PASS = 1024
    COLS = 512
    assert D == DC * P and F == FC * P and VP * SPLIT == V and T < PASS and L <= P and B >= LEAST

    table = nc.dram_tensor("token_table", [T, ROW], F32).ap()
    out_rows = out.rearrange("b l d -> (b l) d")

    with ExitStack() as stack:
        def sb(name, shape, dt=F32):
            return stack.enter_context(nc.sbuf_tensor(name, shape, dt))

        def ps(name, shape, dt=F32):
            return stack.enter_context(nc.psum_tensor(name, shape, dt))

        def sem(name):
            return stack.enter_context(nc.semaphore(name))

        w2_all = sb("w2_all", [P, NE, FC, D])
        w1_sb = sb("w1_sb", [P, 2, DC, F])
        w2_sb = sb("w2_sb", [P, 2, FC, D])
        gate_sb = sb("gate_sb", [P, DC, NE])
        bias_rows = sb("bias_rows", [NE * (FC + DC), P])
        biasT = sb("biasT", [P, NE * (FC + DC)])
        ident = sb("ident", [P, P])
        before = sb("before", [L, P], F16)
        ones16 = sb("ones16", [L, P], F16)
        filler = sb("filler", [L, COLS], F16)
        slot_iota = sb("slot_iota", [L, HALF])
        half_iota = sb("half_iota", [L, NH])
        expert_iota = sb("expert_iota", [L, NE])
        full_tiles = sb("full_tiles", [P, B])
        token_no = sb("token_no", [L, B])
        zeros = sb("zeros", [P, 1 + NE])
        gelu_table = sb("gelu_table", [P, 1])
        x_sb = sb("x_sb", [L, B, D])
        ctx_room = sb("ctx_room", [P, B * SPLIT * D])
        ctx_sb = ctx_room[0:VP, :].rearrange("p (b t d) -> p b t d", t=SPLIT, d=D)
        ctx_stage = sb("ctx_stage", [VP, SPLIT, D])
        ctxT = sb("ctxT", [P, DC, SPLIT * VP])
        stat1 = sb("stat1", [L, B, 6])
        mv1 = sb("mv1", [L, B, 2])
        var1 = sb("var1", [L, B])
        rstd1 = sb("rstd1", [L, B])
        var2 = sb("var2", [L, 1])
        mv2 = sb("mv2", [L, 2])
        power = sb("power", [L, B])
        xn = sb("xn", [L, D])
        xnT = sb("xnT", [P, DC, L])
        nmax = sb("nmax", [L, 1])
        probs = sb("probs", [L, SPLIT * VP])
        prob_sum = sb("prob_sum", [L, 1])
        prob_rec = sb("prob_rec", [L, 1])
        probsT = sb("probsT", [VP, SPLIT, L])
        tok = sb("tok", [L, B, ROW])
        stat2 = sb("stat2", [L, 6])
        x2n = sb("x2n", [L, D])
        x2T = sb("x2T", [P, DC, L])
        lmax = sb("lmax", [L, B])
        shifted = sb("shifted", [L, B, NE])
        lexp = sb("lexp", [L, B, NE])
        lsum = sb("lsum", [L, B])
        weight = sb("weight", [L, B])
        is_max = sb("is_max", [L, B, NE])
        keyed = sb("keyed", [L, B, NE])
        key = sb("key", [L, B])
        chosen = sb("chosen", [L, B, NE], F16)
        more = sb("more", [P, NE, B])
        ntiles = sb("ntiles", [P, 1 + NE])
        tile_bounds = sb("tile_bounds", [P, 1 + NE])
        tile_start, tile_end = tile_bounds[:, 0:NE], tile_bounds[:, 1:1 + NE]
        place = sb("place", [L, B, NE])
        mine = sb("mine", [L, B, NE])
        pos = sb("pos", [L, B])
        pos_i = sb("pos_i", [L, B], I32)
        half_i = sb("half_i", [L, B], I32)
        slot_f = sb("slot_f", [L, B])
        slot_hot = sb("slot_hot", [L, B, HALF], F16)
        half_hot = sb("half_hot", [L, B, NH])
        half_token = sb("half_token", [L, B, NH], F16)
        weight_parts = sb("weight_parts", [L, B, 3], F16)
        weight_rest = sb("weight_rest", [L, 2, B])
        half_weight = sb("half_weight", [L, B, 3, NH], F16)
        past = sb("past", [1, NX, NE])
        filled_to = sb("filled_to", [1, NE])
        filled_from = sb("filled_from", [1, NX, NE])
        tile_filled_to = sb("tile_filled_to", [1, NX])
        tile_filled = sb("tile_filled", [1, NX])
        tile_wide_i = sb("tile_wide_i", [1, NX], I32)
        tile_expert = sb("tile_expert", [1, NX])
        tile_expert_i = sb("tile_expert_i", [1, NX], I32)
        tiles_left = sb("tiles_left", [1, NE], I32)
        half_left = sb("half_left", [1, NE], I32)
        slot_token = sb("slot_token", [HALF, NH], I32)
        slot_weight = sb("slot_weight", [HALF, NH])
        slot_rest = sb("slot_rest", [HALF, NH])
        rows = sb("rows", [HALF, 2, 2, ROW])
        xs = sb("xs", [HALF, 2, D])
        actT = ctx_room[:, 0:2 * FC * TILE].rearrange("p (q c s) -> p q c s", q=2, s=TILE)
        xsT = ctx_room[:, 2 * FC * TILE:2 * (FC + DC) * TILE].rearrange("p (q c s) -> p q c s", q=2, s=TILE)
        yT = sb("yT", [P, DC, TILE])
        res = sb("res", [HALF, 2, 2, D])
        kept_x1 = sb("kept_x1", [HALF, NH, D])
        gather_from = sb("gather_from", [HALF, 4], I32)
        scatter_to = sb("scatter_to", [HALF, 4], I32)

        bank = [ps(f"bank{i}", [P, COLS]) for i in range(4)]
        pair = [ps(f"pair{i}", [P, 2 * COLS]) for i in range(2)]
        VN = SPLIT * VP
        ctxT_ps = pair[0]
        usual_scores_ps, second_scores_ps = bank[0][0:L, 0:VN], pair[1][0:L, 0:VN]
        probsT_ps = bank[1][0:VP, 0:SPLIT * L]
        values_ps = bank[2][0:L, 0:D]
        xnT_ps = bank[3][:, 0:DC * L]
        x2T_ps = pair[1][:, 0:DC * L]
        logit_ps = pair[1][0:L, COLS:COLS + B * NE]
        rank_ps = bank[0][:, 0:(B + 1) * NE]
        token_ps = bank[1][0:HALF, 0:NH]
        biasT_ps = bank[3][:, 0:NE * (FC + DC)]
        weight_ps = pair[1][0:HALF, COLS:COLS + 3 * NH]
        hid_bank = (pair[0][:, 0:COLS], pair[0][:, COLS:2 * COLS], pair[1][:, 0:COLS])
        PER_BANK = COLS // TILE
        bank_groups = [range(k * PER_BANK, min((k + 1) * PER_BANK, FC)) for k in range(len(hid_bank))]
        assert bank_groups[-1].stop == FC
        yT_bank = (bank[0], bank[2])
        y_ps = bank[1][0:HALF, 0:2 * D]
        xsT_ps = bank[3][:, 0:DC * TILE]

        x_head, x_tail, ctx_head, ctx_second, ctx_third, ctx_tail = (
            sem(n) for n in ("x_head", "x_tail", "ctx_head", "ctx_second", "ctx_third", "ctx_tail"))
        gate_loaded, b1_loaded, b2_loaded = sem("gate_loaded"), sem("b1_loaded"), sem("b2_loaded")
        w1_early = (sem("w1_early0"), sem("w1_early1"))
        w1_fixed = (sem("w1_fixed0"), sem("w1_fixed1"))
        w1_here = sem("w1_here")
        w1_loaded = (sem("w1_loaded0"), sem("w1_loaded1"))
        w2_even, w2_odd = sem("w2_even"), sem("w2_odd")
        w2_here = sem("w2_here")
        w2_staged = sem("w2_staged")
        consts_pool = sem("consts_pool")
        (staged, xn_stat, xn_mv, xn_rstd, xn_ready, ctx_turned, xn_turned, xnT_ready, ctxT_ready, scored, max_ready,
         exp_ready, probs_turned, probsT_ready, valued, rec_ready, x1_ready, x2_stat, x2_mv, x2_rstd, x2_ready,
         x2_turned, x2T_ready, routed, row_stored) = (
            sem(n) for n in ("staged", "xn_stat", "xn_mv", "xn_rstd", "xn_ready", "ctx_turned", "xn_turned", "xnT_ready",
                             "ctxT_ready", "scored", "max_ready", "exp_ready", "probs_turned",
                             "probsT_ready", "valued", "rec_ready", "x1_ready", "x2_stat", "x2_mv", "x2_rstd",
                             "x2_ready", "x2_turned", "x2T_ready", "routed", "row_stored"))
        (route, chosen_ready, ranked, hot_ready, listed, slots_ready, experts_ready, shifted_ready, lexp_ready,
         half_weight_ready, weighed, bias_turned, biasT_ready) = (
            sem(n) for n in ("route", "chosen_ready", "ranked", "hot_ready", "listed", "slots_ready",
                             "experts_ready", "shifted_ready", "lexp_ready", "half_weight_ready",
                             "weighed", "bias_turned", "biasT_ready"))
        (xs_ready, xs_turned, xsT_ready, projected, yT_ready, y_turned, rows_clear, from_ready, to_ready,
         x1_kept) = (
            sem(n) for n in ("xs_ready", "xs_turned", "xsT_ready", "projected", "yT_ready", "y_turned",
                             "rows_clear", "from_ready", "to_ready", "x1_kept"))
        gathered = [[sem(f"gathered{slot}{h}") for h in range(2)] for slot in range(2)]
        scattered = [[sem(f"scattered{slot}{h}") for h in range(2)] for slot in range(2)]
        res_ready = (sem("res_ready0"), sem("res_ready1"))
        hidden = [sem(f"hidden{k}") for k in range(len(hid_bank))]
        gelu_done = [sem(f"gelu_done{k}") for k in range(len(hid_bank))]
        xn_var, x2_var, power_set = sem("xn_var"), sem("x2_var"), sem("power_set")
        mean_kept = sem("mean_kept")

        def after_wait(engine):
            engine.nop(nofuse=True)

        block = stack.enter_context(nc.Block())

        def at_least(n, least):
            return not isinstance(n, int) or n >= least

        def scores_ps(b):
            return second_scores_ps if isinstance(b, int) and b == 1 else usual_scores_ps

        def below(n, end):
            return not isinstance(n, int) or n < end

        def when_before(engine, j, final, n=0):
            known = isinstance(j, int) and j < LEAST - 1 - n
            return nullcontext() if known else engine.If(final > j + n)

        def when_final(engine, j, final):
            return engine.If(final <= j)

        def expert_of(engine, j):
            return engine.value_load(tile_expert_i[0:1, bass.ds(j, 1)], min_val=0, max_val=NE - 1)

        def tiles_but(engine, n):
            return engine.value_load(tiles_left[0:1, NE - n:NE - n + 1], min_val=LEAST - n, max_val=NT - n)

        @block.sync
        def _(sp):
            MAIN = VP - VP % 16
            by_part = ctx_in.rearrange("b (p t) d -> p b t d", t=SPLIT)
            x_v = x.rearrange("b l d -> l b d")
            sp.dma_start(x_sb[:, 0:HEAD, :], x_v[:, 0:HEAD, :]).then_inc(x_head, 16)
            for lo, hi, loaded in ((0, 1, ctx_head), (1, 2, ctx_second), (2, 4, ctx_third), (4, B, ctx_tail)):
                sp.dma_start(ctx_sb[0:MAIN, lo:hi], by_part[0:MAIN, lo:hi]).then_inc(loaded, 16)
                sp.dma_start(ctx_sb[MAIN:VP, lo:hi], by_part[MAIN:VP, lo:hi]).then_inc(loaded, 16)
                if lo == 0:
                    sp.dma_start(x_sb[:, HEAD:B, :], x_v[:, HEAD:B, :]).then_inc(x_tail, 16)
            sp.dma_start(gate_sb[:], gate_w.rearrange("(c p) e -> p c e", p=P)).then_inc(gate_loaded, 16)

            def load_w1(e, slot):
                return sp.dma_start(w1_sb[:, slot], w1[e].rearrange("(c p) f -> p c f", p=P))

            load_w1(0, 0).then_inc(w1_early[0], 16)
            load_w1(1, 1).then_inc(w1_early[1], 16)
            sp.dma_start(bias_rows[0:NE * FC, :], b1.rearrange("e (c p) -> (e c) p", p=P)).then_inc(b1_loaded, 16)
            sp.dma_start(bias_rows[NE * FC:NE * (FC + DC), :], b2.rearrange("e (c p) -> (e c) p", p=P)
                         ).then_inc(b2_loaded, 16)

            def load_w2(e, loaded):
                sp.dma_start(w2_all[:, e], w2[e].rearrange("(c p) d -> p c d", p=P)).then_inc(loaded, 16)

            load_w2(0, w2_even)
            load_w2(1, w2_odd)
            with sp.Fori(1, NE // 2) as i:
                for q, loaded in ((0, w2_even), (1, w2_odd)):
                    sp.wait_ge(loaded, 16 * i)
                    sp.sem_inc(w2_here, 1)
                    load_w2(2 * i + q, loaded)
            for loaded in (w2_even, w2_odd):
                sp.wait_ge(loaded, 16 * (NE // 2))
                sp.sem_inc(w2_here, 1)

            sp.wait_ge(experts_ready, 2)

            def load_tile(j, slot):
                e = expert_of(sp, j)
                if at_least(j, 2):
                    sp.wait_ge(hidden[-1], j - 1)
                load_w1(e, slot).then_inc(w1_loaded[slot], 16)

            sp.wait_ge(gathered[0][1], 16)
            for j in range(2):
                sp.wait_ge(w1_early[j], 16)
                e = expert_of(sp, j)
                with sp.If(e != j):
                    load_w1(e, j).then_inc(w1_fixed[j], 16)
                    sp.wait_ge(w1_fixed[j], 16)
                sp.sem_inc(w1_here, 1)
            final = tiles_but(sp, 1)

            def step(j, slot):
                with when_before(sp, j, final, 1):
                    load_tile(j + 2, slot)

            for j in range(PEELED):
                step(j, j % 2)
            with sp.Fori(PEELED // 2, PAIRS) as i:
                for q in range(2):
                    step(2 * i + q, q)

        @block.gpsimd
        def _(pool):
            pool.memset(ident[:], 0.0).then_inc(consts_pool, 1)
            pool.wait_ge(consts_pool, 1)
            pool.affine_select(out=ident[:], in_=ident[:], compare_op=ALU.not_equal, fill=1.0, base=0,
                               pattern=[[-1, P]], channel_multiplier=1).then_inc(consts_pool, 1)

            def inverse_std2(b):
                pool.wait_ge(x2_var, b + 1)
                pool.tensor_tensor(tok[:, b, D + 1:D + 2], var2[:], power[:, 0:1], ALU.pow).then_inc(x2_rstd, 1)
                pool.tensor_copy(tok[:, b, D:D + 1], mv2[:, 0:1]).then_inc(mean_kept, 1)

            def store(b):
                pool.wait_ge(x1_ready, b + 1)
                pool.wait_ge(mean_kept, b + 1)
                pool.dma_start(table[bass.ts(b, L), :], tok[:, b, :]).then_inc(row_stored, 16)

            pool.wait_ge(power_set, 1)
            pool.wait_ge(xn_var, 1)
            pool.tensor_tensor(rstd1[:, 0:HEAD], var1[:, 0:HEAD], power[:, 0:HEAD], ALU.pow).then_inc(xn_rstd, 1)
            pool.memset(before[:], 1.0).then_inc(consts_pool, 1)
            pool.wait_ge(consts_pool, 3)
            pool.affine_select(out=before[:], in_=before[:], compare_op=ALU.is_gt, fill=0.0, base=0,
                               pattern=[[1, P]], channel_multiplier=-1).then_inc(consts_pool, 1)
            pool.wait_ge(xn_var, 2)
            pool.tensor_tensor(rstd1[:, HEAD:B], var1[:, HEAD:B], power[:, HEAD:B], ALU.pow).then_inc(xn_rstd, 1)
            pool.memset(ones16[:], 1.0).then_inc(consts_pool, 1)
            pool.memset(filler[:], 1.0).then_inc(consts_pool, 1)
            pool.iota(slot_iota[:], [[1, HALF]], base=0, channel_multiplier=0,
                      allow_small_or_imprecise_dtypes=True).then_inc(consts_pool, 1)
            pool.iota(half_iota[:], [[1, NH]], base=0, channel_multiplier=0,
                      allow_small_or_imprecise_dtypes=True).then_inc(consts_pool, 1)
            pool.iota(expert_iota[:], [[1, NE]], base=-NE, channel_multiplier=0,
                      allow_small_or_imprecise_dtypes=True).then_inc(consts_pool, 1)
            pool.iota(full_tiles[:], [[TILE, B]], base=0, channel_multiplier=0,
                      allow_small_or_imprecise_dtypes=True).then_inc(consts_pool, 1)
            pool.iota(token_no[:], [[L, B]], base=-PASS, channel_multiplier=1,
                      allow_small_or_imprecise_dtypes=True).then_inc(consts_pool, 1)
            inverse_std2(0)
            pool.memset(zeros[:], 0.0).then_inc(consts_pool, 1)
            pool.memset(ntiles[:, 0:1], 0.0).then_inc(consts_pool, 1)
            pool.memset(rows[:], 0.0).then_inc(rows_clear, 1)
            store(0)
            with pool.Fori(1, B) as b:
                inverse_std2(b)
                store(b)
            pool.wait_ge(row_stored, 16 * B)
            pool.wait_ge(slots_ready, 1)

            def indices(to, j, made):
                pool.tensor_copy(to, slot_token[:, bass.ds(2 * j, 2)]).then_inc(made, 1)
                pool.wait_ge(made, j + 1)
                after_wait(pool)

            def gather(j, slot, before):
                if at_least(before, 1):
                    for h in range(2):
                        pool.wait_ge(gathered[slot][h], 16 * before)
                    pool.wait_ge(x1_kept, j - 1)
                indices(gather_from[:, bass.ts(slot, 2)], j, from_ready)
                for h in range(2):
                    at = gather_from[:, 2 * slot + h:2 * slot + h + 1]
                    pool.indirect_dma_start(out=rows[:, slot, h, :], out_offset=None, in_=table,
                                            in_offset=bass.IndirectOffsetOnAxis(ap=at, axis=0),
                                            bounds_check=T - 1, oob_is_err=False).then_inc(gathered[slot][h], 16)

            def scatter(j, slot, before):
                if at_least(before, 1):
                    for h in range(2):
                        pool.wait_ge(scattered[slot][h], 16 * before)
                indices(scatter_to[:, bass.ts(slot, 2)], j, to_ready)
                for h in range(2):
                    at = scatter_to[:, 2 * slot + h:2 * slot + h + 1]
                    pool.wait_ge(res_ready[h], j + 1)
                    after_wait(pool)
                    pool.indirect_dma_start(out=out_rows, in_=res[:, slot, h, :], in_offset=None,
                                            out_offset=bass.IndirectOffsetOnAxis(ap=at, axis=0),
                                            bounds_check=T - 1, oob_is_err=False).then_inc(scattered[slot][h], 16)

            pool.wait_ge(rows_clear, 1)
            gather(0, 0, 0)
            gather(1, 1, 0)
            pool.wait_ge(experts_ready, 3)
            final = tiles_but(pool, 1)
            gather(2, 0, 1)

            def step(j, slot, pair):
                with when_before(pool, j, final, 2):
                    gather(j + 3, 1 - slot, pair + 1 + slot)
                if at_least(j, 1):
                    scatter(j - 1, 1 - slot, pair - 1 + slot)

            for j in range(PEELED):
                step(j, j % 2, j // 2)
            with pool.Fori(PEELED // 2, PAIRS) as i:
                with pool.If(final >= 2 * i):
                    for q in range(2):
                        j = 2 * i + q
                        with pool.If(final >= j):
                            step(j, q, i)
                            with when_final(pool, j, final):
                                scatter(j, q, i)
                            after_wait(pool)
                    after_wait(pool)
            after_wait(pool)
            tiles = [1 + pool.value_load(half_left[0:1, NE - 1 - slot:NE - slot], min_val=(LEAST - 1 - slot) // 2,
                                         max_val=(NT - 1 - slot) // 2) for slot in range(2)]
            for slot in range(2):
                for h in range(2):
                    pool.wait_ge(scattered[slot][h], 16 * tiles[slot])

        @block.tensor
        def _(pe):
            def turn(b):
                if not at_least(b, DIRECT):
                    pe.wait_ge((ctx_head, ctx_second, ctx_third, ctx_third)[b], 32)
                    context = ctx_sb[:, b]
                else:
                    pe.wait_ge(staged, b - DIRECT + 1)
                    context = ctx_stage
                if at_least(b, 1):
                    pe.wait_ge(ctxT_ready, 2 * b)
                for c in range(DC):
                    for t in range(SPLIT):
                        last = pe.transpose(ctxT_ps[:, c * COLS + t * VP:c * COLS + (t + 1) * VP],
                                            context[:, t, bass.ts(c, P)], ident[0:VP, 0:VP])
                last.then_inc(ctx_turned, 1)
                pe.wait_ge(xn_ready, b + 1)
                for c in range(DC):
                    last = pe.transpose(xnT_ps[:, bass.ts(c, L)], xn[:, bass.ts(c, P)], ident[0:L, 0:L])
                last.then_inc(xn_turned, 1)

            def score(b):
                pe.wait_ge(ctxT_ready, 2 * b + 2)
                pe.wait_ge(xnT_ready, b + 1)
                for c in range(DC):
                    last = pe.matmul(scores_ps(b), xnT[:, c, :], ctxT[:, c, :], start=(c == 0), stop=(c == DC - 1))
                last.then_inc(scored, 1)

            def turn_probs(b):
                pe.wait_ge(exp_ready, b + 1)
                for t in range(SPLIT):
                    last = pe.transpose(probsT_ps[:, bass.ts(t, L)], probs[:, bass.ts(t, VP)], ident[0:L, 0:L])
                last.then_inc(probs_turned, 1)

            def value(b):
                pe.wait_ge(probsT_ready, b + 1)
                if at_least(b, 1):
                    pe.wait_ge(x1_ready, b)
                for t in range(SPLIT):
                    last = pe.matmul(values_ps, probsT[:, t, :], ctx_sb[:, b, t, :],
                                     start=(t == 0), stop=(t == SPLIT - 1))
                last.then_inc(valued, 1)

            def turn_x2(b):
                pe.wait_ge(x2_ready, b + 1)
                for c in range(DC):
                    last = pe.transpose(x2T_ps[:, bass.ts(c, L)], x2n[:, bass.ts(c, P)], ident[0:L, 0:L])
                last.then_inc(x2_turned, 1)

            def router(b):
                pe.wait_ge(x2T_ready, b + 1)
                for c in range(DC):
                    last = pe.matmul(logit_ps[:, bass.ds(b * NE, NE)], x2T[:, c, :], gate_sb[:, c, :],
                                     start=(c == 0), stop=(c == DC - 1))
                last.then_inc(routed, 1)

            def step(b):
                turn_probs(b)
                if at_least(b, 1) and below(b + 1, B):
                    score(b + 1)
                if below(b + 2, B):
                    turn(b + 2)
                value(b)
                if at_least(b - 2, 0):
                    router(b - 2)
                if at_least(b - 1, 0):
                    turn_x2(b - 1)

            def keep_busy(banks):
                for to in banks:
                    pe.matmul(to[:, 0:COLS], ones16[:], filler[:], start=True, stop=True)

            pe.wait_ge(consts_pool, 2)
            with pe.Fori(0, 2):
                for _ in range(8):
                    pe.transpose(pair[1][:, 0:P], ident[:], ident[:])
            turn(0)
            score(0)
            turn(1)
            score(1)
            step(0)
            step(1)
            pe.wait_ge(gate_loaded, 16)
            pe.wait_ge(consts_pool, CONSTS)
            with pe.Fori(2, B - 2) as b:
                step(b)
            step(B - 2)
            step(B - 1)
            keep_busy(3 * hid_bank[0:1])
            router(B - 2)
            keep_busy(7 * hid_bank[0:1])
            turn_x2(B - 1)
            keep_busy(3 * hid_bank[0:1])
            router(B - 1)

            pe.wait_ge(b1_loaded, 16)
            pe.wait_ge(b2_loaded, 16)
            pe.transpose(biasT_ps, bias_rows[:], ident[0:NE * (FC + DC), 0:NE * (FC + DC)]).then_inc(bias_turned, 1)

            keep_busy(7 * hid_bank[0:1])

            pe.wait_ge(chosen_ready, 1)
            flat = chosen[:].rearrange("p b e -> p (b e)")
            pe.matmul(rank_ps[:, 0:B * NE], before[:], flat, start=True, stop=False, skip_group_check=True)
            for s in range(1, B + 1):
                last = pe.matmul(rank_ps[:, s * NE:(B + 1) * NE], ones16[:], flat[:, 0:(B + 1 - s) * NE],
                                 start=False, stop=(s == B), skip_group_check=True)
            last.then_inc(ranked, 1)

            keep_busy(20 * hid_bank[0:1])

            pe.wait_ge(hot_ready, 1)
            for b in range(B):
                last = pe.matmul(token_ps, slot_hot[:, b, :], half_token[:, b, :],
                                 start=(b == 0), stop=(b == B - 1))
            last.then_inc(listed, 1)

            keep_busy(10 * hid_bank[0:1])

            pe.wait_ge(half_weight_ready, 1)
            for b in range(B):
                last = pe.matmul(weight_ps, slot_hot[:, b, :], half_weight[:, b, :, :],
                                 start=(b == 0), stop=(b == B - 1))
            last.then_inc(weighed, 1)

            keep_busy(2 * (*hid_bank, *yT_bank))

            def turn_xs(j):
                pe.wait_ge(xs_ready, j + 1)
                for h in range(2):
                    for c in range(DC):
                        last = pe.transpose(xsT_ps[:, c * TILE + h * HALF:c * TILE + (h + 1) * HALF],
                                            xs[:, h, bass.ts(c, P)], ident[0:HALF, 0:HALF])
                last.then_inc(xs_turned, 1)

            def layer1(j, slot, loads):
                def products(n):
                    if isinstance(loads, int) and loads == 0:
                        pe.wait_ge(w1_here, j + 1)
                    else:
                        pe.wait_ge(w1_loaded[slot], 16 * loads)
                    pe.wait_ge(xsT_ready, j + 1)
                    for k, groups in enumerate(bank_groups):
                        if not at_least(j, 1) and k == len(bank_groups) - 1:
                            turn_xs(1)
                        if at_least(j, 1):
                            pe.wait_ge(gelu_done[k], j)
                        for f in groups:
                            at = (f - groups.start) * TILE
                            for c in range(DC):
                                last = pe.matmul(hid_bank[k][:, at:at + n], w1_sb[:, slot, c, bass.ts(f, P)],
                                                 xsT[:, slot, c, 0:n], start=(c == 0), stop=(c == DC - 1))
                        last.then_inc(hidden[k], 1)
                by_width(j, products)

            def layer2(j, slot):
                def products(n):
                    pe.wait_ge(w2_staged, j + 1)
                    for k in range(len(hid_bank)):
                        pe.wait_ge(gelu_done[k], j + 1)
                    for c in range(DC):
                        if c == DC // 2 and at_least(j, 1):
                            turn_y(j - 1)
                        if at_least(j, 1):
                            pe.wait_ge(yT_ready, DC * (j - 1) + c + 1)
                        for f in range(FC):
                            last = pe.matmul(yT_bank[c][:, 0:n], w2_sb[:, slot, f, bass.ts(c, P)],
                                             actT[:, slot, f, 0:n], start=(f == 0), stop=(f == FC - 1))
                        last.then_inc(projected, 1)
                by_width(j, products)

            def by_width(j, products):
                wide = pe.value_load(tile_wide_i[0:1, bass.ds(j, 1)], min_val=0, max_val=1)
                with pe.If(wide > 0):
                    products(TILE)
                with pe.Else():
                    products(P)

            def turn_y(j):
                if at_least(j, 1):
                    for h in range(2):
                        pe.wait_ge(res_ready[h], j)
                for c in range(DC):
                    pe.wait_ge(yT_ready, DC * j + c + 1)
                    for h in range(2):
                        last = pe.transpose(y_ps[:, h * D + c * P:h * D + (c + 1) * P],
                                            yT[:, c, h * HALF:(h + 1) * HALF], ident[:])
                last.then_inc(y_turned, 1)

            pe.wait_ge(experts_ready, 3)
            final = tiles_but(pe, 1)
            pe.wait_ge(biasT_ready, 1)
            turn_xs(0)
            layer1(0, 0, 0)
            layer1(1, 1, 0)
            turn_xs(2)
            layer2(0, 0)

            def step(j, slot, pair):
                with when_before(pe, j, final):
                    layer1(j + 1, 1 - slot, pair + slot)
                    with when_before(pe, j, final, 1):
                        turn_xs(j + 2)
                    after_wait(pe)
                layer2(j, slot)

            for j in range(1, PEELED):
                step(j, j % 2, j // 2)
            with pe.Fori(PEELED // 2, PAIRS) as i:
                with pe.If(final >= 2 * i):
                    for q in range(2):
                        j = 2 * i + q
                        with pe.If(final >= j):
                            step(j, q, i)
                            with when_final(pe, j, final):
                                turn_y(j)
                            after_wait(pe)
                    after_wait(pe)

        @block.scalar
        def _(sc):
            def ctx_back(b):
                sc.wait_ge(ctx_turned, b + 1)
                if at_least(b, 1):
                    sc.wait_ge(scored, b)
                for c in range(DC):
                    sc.activation(ctxT[:, c, :], ctxT_ps[:, c * COLS:c * COLS + VN], ACT.Copy).then_inc(ctxT_ready, 1)

            def xn_back(b):
                sc.wait_ge(xn_turned, b + 1)
                sc.activation(xnT[:].rearrange("p c l -> p (c l)"), xnT_ps, ACT.Copy).then_inc(xnT_ready, 1)

            def exps(b):
                if at_least(b, 1):
                    sc.wait_ge(rec_ready, b)
                sc.wait_ge(max_ready, b + 1)
                sc.activation(probs[:], scores_ps(b), ACT.Exp, bias=nmax[:], scale=1.0,
                              accum_out=prob_sum[:]).then_inc(exp_ready, 1)

            def probs_back(b):
                sc.wait_ge(probs_turned, b + 1)
                sc.activation(probsT[:].rearrange("p t l -> p (t l)"), probsT_ps, ACT.Copy).then_inc(probsT_ready, 1)

            def x2_back(b):
                sc.wait_ge(x2_turned, b + 1)
                sc.activation(x2T[:].rearrange("p c l -> p (c l)"), x2T_ps, ACT.Copy).then_inc(x2T_ready, 1)

            def step(b):
                probs_back(b)
                if below(b + 1, B):
                    exps(b + 1)
                if below(b + 2, B):
                    ctx_back(b + 2)
                    xn_back(b + 2)
                if at_least(b - 1, 0):
                    x2_back(b - 1)

            ctx_back(0)
            ctx_back(1)
            xn_back(1)
            exps(0)
            step(0)
            step(1)
            with sc.Fori(2, B - 2) as b:
                step(b)
            step(B - 2)
            step(B - 1)
            x2_back(B - 1)

            sc.wait_ge(shifted_ready, 1)
            sc.activation(lexp[:], shifted[:], ACT.Exp).then_inc(lexp_ready, 1)
            sc.wait_ge(bias_turned, 1)
            sc.activation(biasT[:], biasT_ps, ACT.Copy).then_inc(biasT_ready, 1)
            sc.activation(gelu_table[:], zeros[:, 0:1], ACT.Gelu)

            def gelus(j, slot):
                e = expert_of(sc, j)
                for k, groups in enumerate(bank_groups):
                    sc.wait_ge(hidden[k], j + 1)
                    if k == 0 and at_least(j, 2):
                        sc.wait_ge(projected, DC * (j - 1))
                    for f in groups:
                        at = (f - groups.start) * TILE
                        last = sc.activation(actT[:, slot, f, :], hid_bank[k][:, at:at + TILE], ACT.Gelu,
                                             bias=biasT[:, bass.ds(e * FC + f, 1)], scale=1.0)
                    last.then_inc(gelu_done[k], 1)

            def y_back(j):
                e = expert_of(sc, j)
                if at_least(j, 1):
                    sc.wait_ge(y_turned, j)
                for c in range(DC):
                    sc.wait_ge(projected, DC * j + c + 1)
                    sc.activation(yT[:, c, :], yT_bank[c][:, 0:TILE], ACT.Identity,
                                  bias=biasT[:, bass.ds(e * DC + NE * FC + c, 1)], scale=1.0).then_inc(yT_ready, 1)

            sc.wait_ge(biasT_ready, 1)
            sc.wait_ge(experts_ready, 3)
            final = tiles_but(sc, 1)
            gelus(0, 0)

            def step(j, slot):
                with when_before(sc, j, final):
                    gelus(j + 1, 1 - slot)
                y_back(j)

            for j in range(PEELED):
                step(j, j % 2)
            with sc.Fori(PEELED // 2, PAIRS) as i:
                with sc.If(final >= 2 * i):
                    for q in range(2):
                        j = 2 * i + q
                        with sc.If(final >= j):
                            step(j, q)
                    after_wait(sc)

        @block.vector
        def _(dve):
            def statistics(lo, hi):
                for b in range(lo, hi):
                    dve.bn_stats(stat1[:, b, :], x_sb[:, b, :]).then_inc(xn_stat, 1)
                for b in range(lo, hi):
                    dve.wait_ge(xn_stat, b + 1)
                    dve.bn_aggr(mv1[:, b, :], stat1[:, b, :]).then_inc(xn_mv, 1)
                dve.wait_ge(xn_mv, hi)
                dve.tensor_scalar(var1[:, lo:hi], mv1[:, lo:hi, 1], EPS, None, ALU.add).then_inc(xn_var, 1)

            def normalise(b):
                if at_least(b, 1):
                    dve.wait_ge(xn_turned, b)
                dve.tensor_scalar(xn[:], x_sb[:, b, :], mv1[:, b, 0:1], rstd1[:, bass.ds(b, 1)], ALU.subtract,
                                  ALU.mult).then_inc(xn_ready, 1)

            def stage(b):
                if at_least(b, DIRECT + 1):
                    dve.wait_ge(ctx_turned, b)
                dve.tensor_copy(ctx_stage[:], ctx_sb[:, b]).then_inc(staged, 1)

            def score_max(b):
                dve.wait_ge(scored, b + 1)
                dve.tensor_reduce(nmax[:], scores_ps(b), AX, ALU.max, negate=True).then_inc(max_ready, 1)

            def reciprocal_sum(b):
                dve.wait_ge(exp_ready, b + 1)
                dve.reciprocal(prob_rec[:], prob_sum[:]).then_inc(rec_ready, 1)

            def residual(b):
                dve.wait_ge(rec_ready, b + 1)
                dve.wait_ge(valued, b + 1)
                dve.scalar_tensor_tensor(out=tok[:, b, 0:D], in0=values_ps, scalar=prob_rec[:, 0:1],
                                         in1=x_sb[:, b, :], op0=ALU.mult, op1=ALU.add).then_inc(x1_ready, 1)
                dve.wait_ge(x1_ready, b + 1)
                after_wait(dve)
                dve.bn_stats(stat2[:], tok[:, b, 0:D]).then_inc(x2_stat, 1)
                dve.wait_ge(x2_stat, b + 1)
                if at_least(b, 1):
                    dve.wait_ge(mean_kept, b)
                after_wait(dve)
                dve.bn_aggr(mv2[:], stat2[:]).then_inc(x2_mv, 1)
                dve.wait_ge(x2_mv, b + 1)
                dve.tensor_scalar(var2[:], mv2[:, 1:2], EPS, None, ALU.add).then_inc(x2_var, 1)

            def normalise2(b):
                dve.wait_ge(x2_rstd, b + 1)
                if at_least(b, 1):
                    dve.wait_ge(x2_turned, b)
                dve.tensor_scalar(x2n[:], tok[:, b, 0:D], mv2[:, 0:1], tok[:, b, D + 1:D + 2], ALU.subtract,
                                  ALU.mult).then_inc(x2_ready, 1)

            def step(b):
                reciprocal_sum(b)
                if below(b + 1, B):
                    score_max(b + 1)
                if at_least(b - 1, 0):
                    normalise2(b - 1)
                if below(b + 3, B):
                    if at_least(b + 3, DIRECT):
                        stage(b + 3)
                    normalise(b + 3)
                residual(b)

            dve.memset(power[:], -0.5).then_inc(power_set, 1)
            dve.wait_ge(x_head, 16)
            statistics(0, HEAD)
            dve.wait_ge(xn_rstd, 1)
            normalise(0)
            dve.wait_ge(xn_turned, 1)
            dve.tensor_copy(xnT[:].rearrange("p c l -> p (c l)"), xnT_ps).then_inc(xnT_ready, 1)
            normalise(1)
            dve.wait_ge(x_tail, 16)
            statistics(HEAD, B)
            score_max(0)
            dve.wait_ge(xn_rstd, 2)
            normalise(2)
            step(0)
            dve.wait_ge(ctx_tail, 32)
            step(1)
            step(2)
            with dve.Fori(3, B - 3) as b:
                step(b)
            for b in range(B - 3, B):
                step(b)
            normalise2(B - 1)

            steps = 0

            def result(ins):
                nonlocal steps
                steps += 1
                ins.then_inc(route, 1)
                return steps

            def over(ap, n):
                return ap.unsqueeze(2).to_broadcast([ap.shape[0], ap.shape[1], n])

            def under(ap, n):
                return ap.unsqueeze(1).to_broadcast([ap.shape[0], n, ap.shape[1]])

            logits = logit_ps.rearrange("p (b e) -> p b e", e=NE)
            dve.wait_ge(routed, B)
            s = result(dve.tensor_reduce(lmax[:], logits, AX, ALU.max))
            dve.wait_ge(consts_pool, CONSTS)
            dve.wait_ge(route, s)
            s = result(dve.tensor_tensor(is_max[:], logits, over(lmax[:], NE), ALU.is_ge))
            dve.wait_ge(route, s)
            s = result(dve.tensor_tensor(keyed[:], is_max[:], under(expert_iota[:], B), ALU.mult))
            dve.wait_ge(route, s)
            s = result(dve.tensor_reduce(key[:], keyed[:], AX, ALU.min))
            dve.wait_ge(route, s)
            dve.tensor_tensor(chosen[:], under(expert_iota[:], B), over(key[:], NE), ALU.is_equal).then_inc(chosen_ready, 1)
            dve.tensor_tensor(shifted[:], logits, over(lmax[:], NE), ALU.subtract).then_inc(shifted_ready, 1)
            dve.wait_ge(ranked, 1)
            s = result(dve.tensor_tensor(more[:], over(rank_ps[:, B * NE:(B + 1) * NE], B), under(full_tiles[:], NE),
                                         ALU.is_gt))
            dve.wait_ge(route, s)
            s = result(dve.tensor_reduce(ntiles[:, 1:1 + NE], more[:], AX, ALU.add))
            dve.wait_ge(route, s)
            dve.wait_ge(lexp_ready, 1)
            result(dve.tensor_reduce(lsum[:], lexp[:], AX, ALU.add))
            s = result(dve.tensor_tensor_scan(tile_bounds[:], ntiles[:], zeros[:], 0.0, ALU.add, ALU.add))
            dve.wait_ge(route, s)
            result(dve.reciprocal(weight[:], lsum[:]))
            s = result(dve.scalar_tensor_tensor(out=place[:], in0=under(tile_start[0:L, :], B), scalar=float(TILE),
                                                in1=rank_ps[0:L, 0:B * NE].rearrange("p (b e) -> p b e", e=NE),
                                                op0=ALU.mult, op1=ALU.add))
            dve.wait_ge(route, s)
            dve.wait_ge(chosen_ready, 1)
            result(dve.tensor_copy(weight_parts[:, :, 0], weight[:]))
            s = result(dve.tensor_tensor(mine[:], place[:], chosen[:], ALU.mult))
            dve.wait_ge(route, s)
            result(dve.tensor_tensor(weight_rest[:, 0, :], weight[:], weight_parts[:, :, 0], ALU.subtract))
            s = result(dve.tensor_reduce(pos[:], mine[:], AX, ALU.add))
            dve.wait_ge(route, s)
            result(dve.tensor_scalar(weight_parts[:, :, 1], weight_rest[:, 0, :], SCALE, None, ALU.mult))
            s = result(dve.tensor_scalar(pos_i[:], pos[:], float(PER_HALF), None, ALU.mult))
            dve.wait_ge(route, s)
            result(dve.scalar_tensor_tensor(out=weight_rest[:, 1, :], in0=weight_rest[:, 0, :], scalar=SCALE,
                                            in1=weight_parts[:, :, 1], op0=ALU.mult, op1=ALU.subtract))
            s = result(dve.tensor_scalar(half_i[:], pos_i[:], SHIFT, None, ALU.logical_shift_right))
            dve.wait_ge(route, s)
            result(dve.tensor_copy(weight_parts[:, :, 2], weight_rest[:, 1, :]))
            result(dve.tensor_tensor(half_hot[:], under(half_iota[:], B), over(half_i[:], NH), ALU.is_equal))
            s = result(dve.scalar_tensor_tensor(out=slot_f[:], in0=half_i[:], scalar=-float(HALF), in1=pos[:],
                                                op0=ALU.mult, op1=ALU.add))
            dve.wait_ge(route, s)
            dve.tensor_tensor(half_token[:], half_hot[:], over(token_no[:], NH), ALU.mult)
            dve.tensor_tensor(slot_hot[:], under(slot_iota[:], B), over(slot_f[:], HALF), ALU.is_equal).then_inc(hot_ready, 1)
            result(dve.scalar_tensor_tensor(out=filled_to[:], in0=tile_start[0:1, :], scalar=float(TILE),
                                            in1=rank_ps[0:1, B * NE:(B + 1) * NE], op0=ALU.mult, op1=ALU.add))
            s = result(dve.tensor_tensor(past[:], over(half_iota[0:1, 0:NX], NE), under(tile_end[0:1, :], NX), ALU.is_ge))
            dve.wait_ge(listed, 1)
            dve.tensor_scalar(slot_token[:], token_ps, float(PASS), None, ALU.add).then_inc(slots_ready, 1)
            dve.wait_ge(route, s)
            s = result(dve.tensor_reduce(tile_expert[:], past[:], AX, ALU.add))
            dve.tensor_scalar(tiles_left[:], expert_iota[0:1, :], tile_end[0:1, NE - 1:NE], None, ALU.add
                              ).then_inc(experts_ready, 1)
            dve.wait_ge(route, s)
            dve.tensor_scalar(tile_expert_i[:], tile_expert[:], float(NE - 1), None, ALU.min).then_inc(experts_ready, 1)
            s = result(dve.scalar_tensor_tensor(out=filled_from[:], in0=past[:], scalar=float(2 * NX * TILE),
                                                in1=under(filled_to[:], NX), op0=ALU.mult, op1=ALU.add))
            dve.wait_ge(route, s)
            s = result(dve.tensor_reduce(tile_filled_to[:], filled_from[:], AX, ALU.min))
            dve.wait_ge(route, s)
            s = result(dve.scalar_tensor_tensor(out=tile_filled[:], in0=half_iota[0:1, 0:NX], scalar=-float(TILE),
                                                in1=tile_filled_to[:], op0=ALU.mult, op1=ALU.add))
            dve.wait_ge(route, s)
            result(dve.tensor_scalar(half_left[:], tiles_left[:], 1, None, ALU.arith_shift_right))
            dve.tensor_scalar(tile_wide_i[:], tile_filled[:], float(P), None, ALU.is_gt).then_inc(experts_ready, 1)
            dve.tensor_tensor(half_weight[:], half_hot[:].unsqueeze(2).to_broadcast([L, B, 3, NH]),
                              weight_parts[:].unsqueeze(3).to_broadcast([L, B, 3, NH]), ALU.mult
                              ).then_inc(half_weight_ready, 1)
            dve.wait_ge(experts_ready, 3)
            final = tiles_but(dve, 1)
            parts = weight_ps.rearrange("p (k j) -> p k j", k=3)
            dve.wait_ge(weighed, 1)
            s = result(dve.tensor_copy(slot_weight[:], parts[:, 2, :]))
            dve.wait_ge(route, s)
            s = result(dve.tensor_tensor(slot_rest[:], slot_weight[:], parts[:, 1, :], ALU.add))
            dve.wait_ge(route, s)
            s = result(dve.scalar_tensor_tensor(out=slot_weight[:], in0=slot_rest[:], scalar=1.0 / SCALE,
                                                in1=parts[:, 0, :], op0=ALU.mult, op1=ALU.add))
            dve.wait_ge(route, s)

            def tile_in(j, slot, before):
                if at_least(j, 1):
                    dve.wait_ge(xs_turned, j)
                for h in range(2):
                    dve.wait_ge(gathered[slot][h], 16 * before + 16)
                    last = dve.tensor_scalar(xs[:, h, :], rows[:, slot, h, 0:D], rows[:, slot, h, D:D + 1],
                                             rows[:, slot, h, D + 1:D + 2], ALU.subtract, ALU.mult)
                last.then_inc(xs_ready, 1)
                dve.tensor_copy(kept_x1[:, bass.ds(2 * j, 2), :], rows[:, slot, :, 0:D]).then_inc(x1_kept, 1)

            def stage_w2(j, slot):
                e = expert_of(dve, j)
                dve.wait_ge(w2_here, e + 1)
                if at_least(j, 2):
                    dve.wait_ge(projected, DC * (j - 1))
                dve.tensor_copy(w2_sb[:, slot].rearrange("p c d -> p (c d)"), w2_all[:, e].rearrange("p c d -> p (c d)")
                                ).then_inc(w2_staged, 1)

            def xs_back(j, slot):
                dve.wait_ge(xs_turned, j + 1)
                if at_least(j, 2):
                    dve.wait_ge(hidden[-1], j - 1)
                dve.tensor_copy(xsT[:, slot].rearrange("p c s -> p (c s)"), xsT_ps).then_inc(xsT_ready, 1)

            def result_out(j, slot, before):
                dve.wait_ge(x1_kept, j + 1)
                for h in range(2):
                    if at_least(before, 1):
                        dve.wait_ge(scattered[slot][h], 16 * before)
                    if h == 0:
                        dve.wait_ge(y_turned, j + 1)
                    dve.scalar_tensor_tensor(out=res[:, slot, h, :], in0=y_ps[:, bass.ts(h, D)],
                                             scalar=slot_weight[:, bass.ds(2 * j + h, 1)],
                                             in1=kept_x1[:, bass.ds(2 * j + h, 1), :].rearrange("p a d -> p (a d)"),
                                             op0=ALU.mult, op1=ALU.add).then_inc(res_ready[h], 1)

            tile_in(0, 0, 0)
            xs_back(0, 0)
            tile_in(1, 1, 0)
            stage_w2(0, 0)
            xs_back(1, 1)
            tile_in(2, 0, 1)
            stage_w2(1, 1)

            def step(j, slot, pair):
                if at_least(j, 1):
                    with when_before(dve, j, final):
                        stage_w2(j + 1, 1 - slot)
                with when_before(dve, j, final, 1):
                    xs_back(j + 2, slot)
                with when_before(dve, j, final, 2):
                    tile_in(j + 3, 1 - slot, pair + 1 + slot)
                if at_least(j, 1):
                    result_out(j - 1, 1 - slot, pair - 1 + slot)

            for j in range(PEELED):
                step(j, j % 2, j // 2)
            with dve.Fori(PEELED // 2, PAIRS) as i:
                with dve.If(final >= 2 * i):
                    for q in range(2):
                        j = 2 * i + q
                        with dve.If(final >= j):
                            step(j, q, i)
                            with when_final(dve, j, final):
                                result_out(j, q, i)
                            after_wait(dve)
                    after_wait(dve)


_INS = ['x', 'ctx_1024', 'L0_ffn_gate_w', 'L0_ffn_w1', 'L0_ffn_b1', 'L0_ffn_w2', 'L0_ffn_b2']


def kernel(**inputs):
    import numpy as _np
    import concourse.bacc as _bacc
    from concourse.bass_utils import run_bass_kernel_spmd as _run

    nc = _bacc.Bacc("TRN2", target_bir_lowering=False, num_devices=1)
    arrays, args = {}, []
    for name in _INS:
        a = _np.ascontiguousarray(inputs[name])
        arrays[f"in_{name}_dram"] = a
        args.append(nc.dram_tensor(f"in_{name}_dram", a.shape, mybir.dt.from_np(a.dtype), kind="ExternalInput").ap())
    shape = arrays["in_x_dram"].shape
    args.append(nc.dram_tensor("out_0_dram", shape, F32, kind="ExternalOutput").ap())
    xattn_moe(nc, *args)
    r = _run(nc, [arrays], core_ids=[0])
    return r.results[0]["out_0_dram"]
```
